# Optimizing a Trainium2 kernel written in Bass

```python
import numpy as np
import jax
import jax.numpy as jnp

def _softmax(x, axis=-1):
    return jax.nn.softmax(x, axis=axis)

def _gelu(x):
    return jax.nn.gelu(x, approximate=True)

def _silu(x):
    return jax.nn.silu(x)

def _sigmoid(x):
    return jax.nn.sigmoid(x)

def _layernorm(x, axis=-1, eps=1e-05):
    m = jnp.mean(x, axis=axis, keepdims=True)
    v = jnp.var(x, axis=axis, keepdims=True)
    return (x - m) / jnp.sqrt(v + eps)

def _scatter_add(tgt, idx, src, axis=0):
    return tgt.at[idx].add(src)

def _segment_sum(src, seg, n):
    return jax.ops.segment_sum(src, seg, n)
kernel_name = 'mk_adj_preln_d1_adj_r2_e80e70'

def setup_inputs(seed: int=0):
    np.random.seed(seed)
    _w = jnp.asarray

    def _rec_inputs():
        import jax
        import jax.numpy as jnp
        _gk = jax.random.key(seed)
        x = -0.0005207 + 1.001 * jax.random.normal(jax.random.fold_in(_gk, 1), (2048, 256), jnp.float32)
        _w = (1.0 + jnp.arange(2048, dtype=jnp.float32)) ** (-0.5)
        _w = _w / _w.mean()
        _pij = jnp.clip(0.00195312 * _w[:, None] * _w[None, :], 0.0, 1.0)
        _a = jax.random.uniform(jax.random.fold_in(_gk, 2), (2048, 2048)) < _pij
        adj = _a.astype(jnp.int32)
        _nm = jnp.ones((2048,), dtype=bool)
        nodemask = jnp.where(_nm, 1.0, 0.0).astype(jnp.int32)
        return (x, adj, nodemask)
    x, adj, nodemask = _rec_inputs()

    def _L0_gnn_setup():
        import jax, jax.numpy as jnp
        import numpy as np
        D = 256
        H = 8
        HD = D // H
        EPS = 1e-05
        NEG = -1e+30

        def layer_norm(x, scale, bias):
            mu = jnp.mean(x, axis=-1, keepdims=True)
            var = jnp.mean(jnp.square(x - mu), axis=-1, keepdims=True)
            return (x - mu) * jax.lax.rsqrt(var + EPS) * scale + bias
        key = jax.random.key(seed)
        ks = jax.random.split(key, 16)
        S = T = 2048
        inp = {'h_source': jax.random.normal(ks[0], (S, D), jnp.float32), 'h_target': jax.random.normal(ks[1], (T, D), jnp.float32), 'edge_mask': jax.random.randint(ks[2], (T, S), 0, 2, jnp.int32), 'source_mask': jnp.ones((S,), jnp.int32), 'target_mask': jnp.ones((T,), jnp.int32), 'ln1_scale': jnp.ones((D,), jnp.float32), 'ln1_bias': jnp.zeros((D,), jnp.float32), 'Wq': jax.random.normal(ks[3], (D, D), jnp.float32) / np.sqrt(D), 'bq': jnp.zeros((D,), jnp.float32), 'Wk': jax.random.normal(ks[4], (D, D), jnp.float32) / np.sqrt(D), 'bk': jnp.zeros((D,), jnp.float32), 'Wv': jax.random.normal(ks[5], (D, D), jnp.float32) / np.sqrt(D), 'bv': jnp.zeros((D,), jnp.float32), 'Wo': jax.random.normal(ks[6], (D, D), jnp.float32) / np.sqrt(D), 'bo': jnp.zeros((D,), jnp.float32), 'ln2_scale': jnp.ones((D,), jnp.float32), 'ln2_bias': jnp.zeros((D,), jnp.float32), 'W1': jax.random.normal(ks[7], (D, 4 * D), jnp.float32) / np.sqrt(D), 'W2': jax.random.normal(ks[8], (4 * D, D), jnp.float32) / np.sqrt(4 * D)}
        return inp
    _L0_gnn_all = _L0_gnn_setup()
    _L0_gnn_in = {k: v for k, v in _L0_gnn_all.items() if k in ('h_target', 'ln1_scale', 'ln1_bias', 'Wq', 'bq', 'Wk', 'bk', 'Wv', 'bv', 'Wo', 'bo', 'ln2_scale', 'ln2_bias', 'W1', 'W2')}
    del _L0_gnn_all
    return {'x': x, 'adj': adj, 'nodemask': nodemask, 'L0_gnn_h_target': _L0_gnn_in['h_target'], 'L0_gnn_ln1_scale': _L0_gnn_in['ln1_scale'], 'L0_gnn_ln1_bias': _L0_gnn_in['ln1_bias'], 'L0_gnn_Wq': _L0_gnn_in['Wq'], 'L0_gnn_bq': _L0_gnn_in['bq'], 'L0_gnn_Wk': _L0_gnn_in['Wk'], 'L0_gnn_bk': _L0_gnn_in['bk'], 'L0_gnn_Wv': _L0_gnn_in['Wv'], 'L0_gnn_bv': _L0_gnn_in['bv'], 'L0_gnn_Wo': _L0_gnn_in['Wo'], 'L0_gnn_bo': _L0_gnn_in['bo'], 'L0_gnn_ln2_scale': _L0_gnn_in['ln2_scale'], 'L0_gnn_ln2_bias': _L0_gnn_in['ln2_bias'], 'L0_gnn_W1': _L0_gnn_in['W1'], 'L0_gnn_W2': _L0_gnn_in['W2']}

def reference(x, adj, nodemask, L0_gnn_h_target, L0_gnn_ln1_scale, L0_gnn_ln1_bias, L0_gnn_Wq, L0_gnn_bq, L0_gnn_Wk, L0_gnn_bk, L0_gnn_Wv, L0_gnn_bv, L0_gnn_Wo, L0_gnn_bo, L0_gnn_ln2_scale, L0_gnn_ln2_bias, L0_gnn_W1, L0_gnn_W2):
    import jax
    import jax.numpy as jnp

    def _L0_gnn_ref(h_source, h_target, edge_mask, source_mask, target_mask, ln1_scale, ln1_bias, Wq, bq, Wk, bk, Wv, bv, Wo, bo, ln2_scale, ln2_bias, W1, W2):
        import jax, jax.numpy as jnp
        import numpy as np
        D = 256
        H = 8
        HD = D // H
        EPS = 1e-05
        NEG = -1e+30

        def layer_norm(x, scale, bias):
            mu = jnp.mean(x, axis=-1, keepdims=True)
            var = jnp.mean(jnp.square(x - mu), axis=-1, keepdims=True)
            return (x - mu) * jax.lax.rsqrt(var + EPS) * scale + bias
        smask = (source_mask == 1)[:, None]
        tmask = (target_mask == 1)[:, None]
        hs = layer_norm(h_source, ln1_scale, ln1_bias)
        ht = layer_norm(h_target, ln1_scale, ln1_bias)
        hs = jnp.where(smask, hs, 0.0)
        ht = jnp.where(tmask, ht, 0.0)
        T, S = (ht.shape[0], hs.shape[0])
        q = (ht @ Wq + bq).reshape(T, H, HD) / jnp.sqrt(jnp.float32(HD))
        k = (hs @ Wk + bk).reshape(S, H, HD)
        v = (hs @ Wv + bv).reshape(S, H, HD)
        logits = jnp.einsum('thd,shd->hts', q, k)
        logits = jnp.where(edge_mask[None] != 0, logits, NEG)
        probs = jax.nn.softmax(logits, axis=-1)
        ctx = jnp.einsum('hts,shd->thd', probs, v).reshape(T, D)
        attn = ctx @ Wo + bo
        attn = jnp.where(tmask, attn, 0.0)
        ht = ht + attn
        ht = layer_norm(ht, ln2_scale, ln2_bias)
        ht = jnp.where(tmask, ht, 0.0)
        ff = jax.nn.gelu(ht @ W1) @ W2
        return ht + ff
    h = jnp.maximum(_layernorm(x, axis=-1), 0.0)
    x = x + _L0_gnn_ref(h, L0_gnn_h_target, adj, nodemask, nodemask, L0_gnn_ln1_scale, L0_gnn_ln1_bias, L0_gnn_Wq, L0_gnn_bq, L0_gnn_Wk, L0_gnn_bk, L0_gnn_Wv, L0_gnn_bv, L0_gnn_Wo, L0_gnn_bo, L0_gnn_ln2_scale, L0_gnn_ln2_bias, L0_gnn_W1, L0_gnn_W2)
    return x

_drawn_inputs = setup_inputs


def setup_inputs(seed=0):
    import zlib

    import numpy as np

    out = dict(_drawn_inputs(seed))
    spreads = {'L0_gnn_ln1_scale': (1.0, 0.2),
     'L0_gnn_ln1_bias': (0.0, 0.1),
     'L0_gnn_bq': (0.0, 0.455),
     'L0_gnn_bk': (0.0, 0.8),
     'L0_gnn_bv': (0.0, 0.1),
     'L0_gnn_bo': (0.0, 0.1),
     'L0_gnn_ln2_scale': (1.0, 0.2),
     'L0_gnn_ln2_bias': (0.0, 0.1)}
    factors = {}
    for name, (base, spread) in spreads.items():
        noise = np.random.default_rng([zlib.crc32(name.encode()), seed]).standard_normal(out[name].shape)
        drawn = base * np.exp(spread * noise) if base else spread * noise
        out[name] = jnp.asarray(drawn.astype(out[name].dtype))
    for name, factor in factors.items():
        out[name] = (out[name] * factor).astype(out[name].dtype)
    return out
```

```python
from contextlib import ExitStack

import concourse.bass as bass
from concourse import mybir

ALU = mybir.AluOpType
ACT = mybir.ActivationFunctionType
F32 = mybir.dt.float32
F32R = mybir.dt.float32r
I32 = mybir.dt.int32

P = 128
N = 2048
D = 256
H = 8
HD = D // H
F = 4 * D
EPS = 1e-5
NEG = 1e30
HUGE = 3e38
QSCALE = -float(HD) ** -0.5

NB = N // P
DC = D // P
FC = F // P
GT = 512
GB = GT // P
NG = N // GT
HG = P // HD

PAIR = 2 * P
NPAIR = N // PAIR
CH = 1024
UCH = 2 * N // CH
PCH = UCH * H
PAIRS_IN_BODY = 2
BCH = PAIRS_IN_BODY * PCH
BU = PAIRS_IN_BODY * H
TRIPS = NPAIR // PAIRS_IN_BODY

EXP_LAG = 2
T_LAG = 3
PV_LAG = 7
CTX_LAG = 11

PR = 4
MR = 16
CR = 4
FR = 4


def program(nc, x, adj, nodemask, h_target, ln1_scale, ln1_bias, Wq, bq, Wk, bk, Wv, bv, Wo, bo,
            ln2_scale, ln2_bias, W1, W2, out):
    with ExitStack() as ctx:
        def sb(name, shape, dt=F32):
            return ctx.enter_context(nc.sbuf_tensor(name, shape, dt))

        def sem(name):
            return ctx.enter_context(nc.semaphore(name))

        parts_scr = nc.dram_tensor("parts_scr", (2, 2, D, N), F32).ap()
        ctx_scr = nc.dram_tensor("ctx_scr", (H, P, N), F32).ap()
        ht_scr = nc.dram_tensor("ht_scr", (N, D), F32).ap()

        kst = sb("kst", [P, H, N], F32R)
        qst = sb("qst", [P, 2, H, PAIR], F32R)
        vals = sb("vals", [P, NB, D])
        prob = sb("prob", [P, PR, N])
        probT = sb("probT", [P, 2, NB, PAIR])
        mask = sb("mask", [P, 2, 2, N])
        cpart = sb("cpart", [P, CR, PAIR])
        ident = sb("ident", [P, P])
        head_sel = sb("head_sel", [H, D])
        minhalf = sb("minhalf", [P, MR])
        minrow = sb("minrow", [P, MR // 2])
        denhalf = sb("denhalf", [P, 2, 2, 2, H])
        den = sb("den", [P, NB, H])
        rden = sb("rden", [P, NB, H])
        half_neg = sb("half_neg", [P, GB])
        nmask = sb("nmask", [P, NB], I32)
        nmaskf = sb("nmaskf", [P, NB])
        qbias = sb("qbias", [P, DC])
        kbias = sb("kbias", [P, DC])
        qbias_s = sb("qbias_s", [P, DC])
        stats = sb("stats", [P, GB, 6])
        stats2 = sb("stats2", [P, GB, 6])
        mv = sb("mv", [P, 2, GB, 2])
        mv2 = sb("mv2", [P, 2, GB, 2])
        vareps = sb("vareps", [P, 2, GB])
        rstd = sb("rstd", [P, 2, GB])
        rstd1 = sb("rstd1", [P, 2, GB])
        nbias = sb("nbias", [P, 2, GB])
        nbias1 = sb("nbias1", [P, 2, GB])
        tmpa = sb("tmpa", [P, GB])

        xs = prob[:, 0:2, :].rearrange("p a (b d) -> p (a b) d", d=D)
        srcT = prob[:, 2:4, :]
        tgtT = probT[:, 0, :, :].rearrange("p b t -> p (b t)").rearrange("p (c n) -> p c n", c=DC)
        spare = probT[:, 1, :, :].rearrange("p b t -> p (b t)")
        ring_f = spare[:, 0:FR * GT].rearrange("p (r n) -> p r n", r=FR)
        ofs = FR * GT
        s1_bc = spare[:, ofs:ofs + D]
        b1_bc = spare[:, ofs + D:ofs + 2 * D]
        ofs += 2 * D
        wqkv = spare[:, ofs:ofs + 3 * DC * D].rearrange("p (w c n) -> p w c n", w=3, c=DC)
        cspare = cpart[:, :, :].rearrange("p r t -> p (r t)")
        bv_bc = cspare[:, 0:D]
        ring_hl = mask[:, 1, :, :].rearrange("p a n -> p (a n)").bitcast(F32R).rearrange(
            "p (r s n) -> p r s n", r=FR, s=2)

        w1 = mask[:, 0, 0, :].rearrange("p (c f) -> p c f", c=DC)
        w2 = mask[:, 0, 1, :].rearrange("p (c d) -> p c d", c=FC)
        gel = prob[:, :, :].rearrange("p (b a) (c n) -> p b (a c) n", b=2, n=GT)
        cin = probT[:, :, :, :].rearrange("p b s t -> p b (s t)").rearrange(
            "p b (g j n) -> p b g j n", g=DC, j=HG)
        m1 = mask[:, 1, :, :].rearrange("p a n -> p (a n)")
        s2_bc = m1[:, 0:D]
        b2_bc = m1[:, D:2 * D]
        bo_bc = m1[:, 2 * D:3 * D]
        hid = m1[:, 1024:2048].rearrange("p (b d) -> p b d", d=D)
        hidT = m1[:, 2048:3072].rearrange("p (c n) -> p c n", c=DC)
        xres = m1[:, 3072:4096].rearrange("p (b d) -> p b d", d=D)
        ht2 = vals[:, 0:2 * GB, :]
        htin = vals[:, 2 * GB:3 * GB, :]
        cnorm = vals[:, 3 * GB:4 * GB, :].rearrange("p b d -> p (b d)").rearrange("p (c n) -> p c n", c=DC)
        wo = cspare[:, 0:DC * D].rearrange("p (c n) -> p c n", c=DC)
        rdT = cspare[0:H, DC * D:DC * D + GT]

        score = [ctx.enter_context(nc.psum_tensor(f"score{i}", [P, CH], F32)) for i in range(2)]
        trA = ctx.enter_context(nc.psum_tensor("trA", [P, GT], F32))
        trB = ctx.enter_context(nc.psum_tensor("trB", [P, GT], F32))
        pv = [ctx.enter_context(nc.psum_tensor(f"pv{i}", [P, GT], F32)) for i in range(2)]
        bank = [score[0][:, 0:GT], score[0][:, GT:CH], score[1][:, 0:GT], score[1][:, GT:CH],
                trA[:, :], trB[:, :], pv[0][:, :], pv[1][:, :]]

        s_w = sem("weights_loaded")
        s_xin = [sem(f"group_loaded{g}") for g in range(2 * NG)]
        s_adj0 = sem("adj_loaded0")
        s_adj1 = sem("adj_loaded1")
        s_zero = sem("constants_zeroed")
        s_const = sem("constants_ready")
        s_stat = sem("stats_taken")
        s_mv1 = sem("moments_x")
        s_mv2 = sem("moments")
        s_pc = sem("pool_small_step")
        s_r1 = sem("rstd_x_ready")
        s_r2 = sem("rstd_ready")
        s_relu = sem("relu_done")
        s_xn = sem("normalised")
        s_sc = sem("scaled")
        s_ln = sem("ln1_done")
        s_tp = sem("rows_transposed")
        s_tcD = sem("transposes_copied_vector")
        s_tcA = sem("transposes_copied_scalar")
        s_prj = sem("projected")
        s_vp = sem("values_projected")
        s_f = sem("projection_copied")
        s_hi = sem("high_part")
        s_lo = sem("low_part")
        s_ve = sem("values_copied")
        s_parts = [sem(f"parts_stored{r}") for r in range(FR)]
        s_kst = [sem(f"keys_stacked{h}") for h in range(4)]
        s_qst = [sem(f"queries_stacked{b}") for b in range(2)]
        s_hts = sem("targets_stored")
        s_htin = sem("targets_loaded")
        s_m = sem("mask_ready")
        s_qk = sem("scores_ready")
        s_mx = sem("minimum_taken")
        s_nm = sem("minimum_of_row")
        s_exp = sem("exp_done")
        s_trA = sem("transposed_a")
        s_trB = sem("transposed_b")
        s_evA = sem("copied_a")
        s_evB = sem("copied_b")
        s_pv = sem("context_summed")
        s_ctx = sem("context_copied")
        s_cst = [sem(f"context_stored{r}") for r in range(CR)]
        s_den = sem("denominators")
        s_w3 = sem("ffn_weights_loaded")
        s_cin = [sem(f"context_loaded{b}") for b in range(2)]
        s_xr = sem("x_loaded")
        s_rd = sem("reciprocals")
        s_rt = sem("reciprocals_transposed")
        s_rtc = sem("reciprocals_copied")
        s_rb = sem("reciprocals_spread")
        s_add = sem("parts_added_pool")
        s_add2 = sem("parts_added_vector")
        s_cn = sem("context_normalised")
        s_wo = sem("output_projected")
        s_h1 = sem("bias_added")
        s_h2 = sem("residual_added")
        s_st3 = sem("stats_taken3")
        s_mv3 = sem("moments3")
        s_p3 = sem("pool_small_step3")
        s_r3 = sem("rstd3_ready")
        s_n1 = sem("centred3")
        s_n2 = sem("ln2_affine")
        s_n3 = sem("ln2_masked")
        s_t3 = sem("ln2_transposed")
        s_c3 = sem("ln2_copied")
        s_f1 = sem("ffn1_done")
        s_g = sem("gelu_done")
        s_f2 = sem("ffn2_done")
        s_y1 = sem("ffn_added")
        s_y2 = sem("x_added")
        s_out = sem("out_stored")

        def rows(a, g):
            return a.rearrange("(b p) d -> p b d", p=P)[:, g * GB:(g + 1) * GB, :]

        def wait(eng, s, value):
            if isinstance(value, int) and value <= 0:
                return
            eng.wait_ge(s, value)

        block = ctx.enter_context(nc.Block())

        def tokens(g):
            g %= NG
            return xs[:, g * GB:(g + 1) * GB, :]

        def turned(g):
            a = srcT if g < NG else tgtT
            k = g % NG
            return a[:, :, k * GT:(k + 1) * GT]

        TRIPLE = (0, 1, 0, 1), (0, 0, 1, 1)
        KHEADS = [(0, 1), (1, 2), (2, 4), (4, 8)]

        def load_adj(sp, pair, s):
            b = 0 if s is s_adj0 else 1
            sp.dma_start(
                mask[:, b, :, :].bitcast(I32),
                adj[bass.ds(pair * PAIR, PAIR), :].rearrange("(b p) n -> p b n", p=P)).then_inc(s, 16)

        def load_queries(sp, pair, b):
            for quad in range(4):
                sp.dma_start(
                    qst[HD * quad:HD * (quad + 1), b, :, :].bitcast(F32),
                    parts_scr[0, TRIPLE[1][quad], :, bass.ds(pair * PAIR, PAIR)].rearrange(
                        "(h d) n -> d h n", d=HD)).then_inc(s_qst[b], 16)

        @block.sync
        def _(sp):
            sp.dma_start(tokens(0), rows(x, 0)).then_inc(s_xin[0], 16)
            sp.dma_start(nmask[:], nodemask.rearrange("(b p) -> p b", p=P),
                         allow_slow_non_contiguous=True).then_inc(s_w, 16)
            for g in range(1, NG):
                sp.dma_start(tokens(g), rows(x, g)).then_inc(s_xin[g], 16)
            sp.dma_start(s1_bc, ln1_scale.rearrange("(a d) -> a d", a=1).to_broadcast([P, D])).then_inc(s_w, 16)
            sp.dma_start(b1_bc, ln1_bias.rearrange("(a d) -> a d", a=1).to_broadcast([P, D])).then_inc(s_w, 16)
            sp.dma_start(bv_bc, bv.rearrange("(a d) -> a d", a=1).to_broadcast([P, D])).then_inc(s_w, 16)
            for j, w in enumerate((Wq, Wk, Wv)):
                sp.dma_start(wqkv[:, j, :, :], w.rearrange("(c p) n -> p c n", p=P)).then_inc(s_w, 16)
            sp.dma_start(qbias[:], bq.rearrange("(c p) -> p c", p=P),
                         allow_slow_non_contiguous=True).then_inc(s_w, 16)
            sp.dma_start(kbias[:], bk.rearrange("(c p) -> p c", p=P),
                         allow_slow_non_contiguous=True).then_inc(s_w, 16)
            load_adj(sp, 0, s_adj0)
            for s in range(2 * NG * DC):
                which = 1 if s < NG * DC else 0
                g, c = s % (NG * DC) // DC, s % DC
                if which == 1 and c == 0:
                    sp.wait_ge(s_tp, DC * (g + 1))
                    sp.dma_start(tokens(NG + g), rows(h_target, g)).then_inc(s_xin[NG + g], 16)
                if which == 0 and c == 0:
                    sp.wait_ge(s_ln, GB * (NG + g + 1))
                    sp.dma_start(rows(ht_scr, g), tokens(NG + g)).then_inc(s_hts, 16)
                sp.wait_ge(s_lo, s + 1)
                sp.wait_ge(s_hi, s + 1)
                sp.dma_start(
                    parts_scr[which, :, c * P:(c + 1) * P, g * GT:(g + 1) * GT].rearrange("s p n -> p s n"),
                    ring_hl[:, s % FR, :, :].bitcast(F32)).then_inc(s_parts[s % FR], 16)
                if s == NG * DC + FR - 1:
                    for r in range(FR):
                        sp.wait_ge(s_parts[r], 16 * (NG * DC // FR))
                    for k, (h0, h1) in enumerate(KHEADS):
                        for quad in range(4):
                            sp.dma_start(
                                kst[HD * quad:HD * (quad + 1), h0:h1, :].bitcast(F32),
                                parts_scr[1, TRIPLE[0][quad], h0 * HD:h1 * HD, :].rearrange(
                                    "(h d) n -> d h n", d=HD)).then_inc(s_kst[k], 16)
            for r in range(FR):
                sp.wait_ge(s_parts[r], 16 * (2 * NG * DC // FR))
            load_queries(sp, 0, 0)
            load_adj(sp, 1, s_adj1)
            load_queries(sp, 1, 1)

            def unit(i, u):
                p, h = u // H, u % H
                pair = i * PAIRS_IN_BODY + p
                sp.wait_ge(s_ctx, i * BU + u + 1)
                sp.nop(nofuse=True)
                sp.dma_start(ctx_scr[h, :, bass.ds(pair * PAIR, PAIR)], cpart[:, u % CR, :]).then_inc(
                    s_cst[u % CR], 16)

            def refill(i, p):
                pair = i * PAIRS_IN_BODY + p
                sp.wait_ge(s_mx, pair * PCH + PCH)
                sp.nop(nofuse=True)
                load_adj(sp, pair + 2, (s_adj0, s_adj1)[p])
                sp.wait_ge(s_qk, pair * PCH + PCH)
                sp.nop(nofuse=True)
                load_queries(sp, pair + 2, p)

            def body(i, last):
                for u in range(BU):
                    unit(i, u)
                    if u % H == H - 3 and not last:
                        refill(i, u // H)

            body(0, False)
            with sp.Fori(1, TRIPS - 1) as i:
                body(i, False)
            body(TRIPS - 1, True)

            sp.wait_ge(s_mx, (NPAIR - 1) * PCH)
            sp.dma_start(w1, W1.rearrange("(c p) f -> p c f", p=P)).then_inc(s_w3, 16)
            sp.dma_start(w2, W2.rearrange("(c p) d -> p c d", p=P)).then_inc(s_w3, 16)
            sp.wait_ge(s_mx, NPAIR * PCH)
            for dst, src in ((s2_bc, ln2_scale), (b2_bc, ln2_bias), (bo_bc, bo)):
                sp.dma_start(dst, src.rearrange("(a d) -> a d", a=1).to_broadcast([P, D])).then_inc(s_w3, 16)
            for r in range(CR):
                sp.wait_ge(s_cst[r], 16 * (NPAIR * H // CR))
            sp.wait_ge(s_pv, NPAIR * H)

            def load_context(g):
                for c in range(DC):
                    for h in range(HG):
                        sp.dma_start(
                            cin[HD * h:HD * (h + 1), g % 2, c, :, :],
                            ctx_scr[c * HG + h, :, g * GT:(g + 1) * GT].rearrange("(j d) n -> d j n", d=HD)
                        ).then_inc(s_cin[g % 2], 16)

            sp.dma_start(wo, Wo.rearrange("(c p) n -> p c n", p=P)).then_inc(s_w3, 16)
            sp.dma_start(htin, rows(ht_scr, 0)).then_inc(s_htin, 16)
            load_context(0)
            load_context(1)
            for g in range(NG):
                if g >= 1:
                    sp.wait_ge(s_out, 16 * g)
                sp.dma_start(xres, rows(x, g)).then_inc(s_xr, 16)
                if g + 2 < NG:
                    sp.wait_ge(s_cn, (g + 1) * DC)
                    load_context(g + 2)
                if g + 1 < NG:
                    sp.wait_ge(s_h2, GB * (g + 1))
                    sp.dma_start(htin, rows(ht_scr, g + 1)).then_inc(s_htin, 16)
                sp.wait_ge(s_y2, GB * (g + 1))
                sp.dma_start(rows(out, g), xres).then_inc(s_out, 16)
            sp.wait_ge(s_out, 16 * NG)

        @block.gpsimd
        def _(pool):
            pool.memset(ident[:], 0.0).then_inc(s_zero, 1)
            pool.memset(head_sel[:], 0.0).then_inc(s_zero, 1)
            pool.memset(half_neg[:], -0.5).then_inc(s_const, 1)
            pool.wait_ge(s_zero, 2)
            pool.affine_select(out=ident[:], in_=ident[:], compare_op=ALU.not_equal, fill=1.0, base=0,
                               pattern=[[-1, P]], channel_multiplier=1).then_inc(s_const, 1)
            pool.affine_select(out=head_sel[:].rearrange("h (g d) -> h g d", d=HD),
                               in_=head_sel[:].rearrange("h (g d) -> h g d", d=HD),
                               compare_op=ALU.not_equal, fill=1.0, base=0,
                               pattern=[[-1, H], [0, HD]], channel_multiplier=1).then_inc(s_const, 1)
            pool.wait_ge(s_w, 16 * 9)
            pool.tensor_scalar(nmaskf[:], nmask[:], 1.0, None, ALU.is_equal).then_inc(s_const, 1)
            pool.tensor_scalar(qbias_s[:], qbias[:], QSCALE, None, ALU.mult).then_inc(s_const, 1)
            pool.wait_ge(s_const, 5)

            step = [0]

            def small(ins):
                step[0] += 1
                ins.then_inc(s_pc, 1)
                pool.wait_ge(s_pc, step[0])

            def root(var, b, dst):
                small(pool.tensor_scalar(vareps[:, b, :], var, EPS, None, ALU.add))
                small(pool.tensor_tensor(dst, vareps[:, b, :], half_neg[:], ALU.pow))

            def norm_x(g):
                b = g % 2
                pool.wait_ge(s_mv1, GB * (g + 1))
                if g >= 2:
                    pool.wait_ge(s_relu, GB * (g - 1))
                root(mv[:, b, :, 1], b, rstd1[:, b, :])
                small(pool.tensor_tensor(tmpa[:], mv[:, b, :, 0], rstd1[:, b, :], ALU.mult))
                pool.tensor_scalar(nbias1[:, b, :], tmpa[:], -1.0, None, ALU.mult).then_inc(s_r1, 1)
                pool.wait_ge(s_r1, g + 1)

            def norm(g):
                b = g % 2
                k = g % NG
                pool.wait_ge(s_mv2, GB * (g + 1))
                if g >= 2:
                    pool.wait_ge(s_xn, GB * (g - 1))
                root(mv2[:, b, :, 1], b, tmpa[:])
                small(pool.tensor_tensor(rstd[:, b, :], tmpa[:], nmaskf[:, k * GB:(k + 1) * GB], ALU.mult))
                small(pool.tensor_tensor(vareps[:, b, :], mv2[:, b, :, 0], rstd[:, b, :], ALU.mult))
                pool.tensor_scalar(nbias[:, b, :], vareps[:, b, :], -1.0, None, ALU.mult).then_inc(s_r2, 1)
                pool.wait_ge(s_r2, g + 1)

            def scale(g):
                for j in range(GB):
                    pool.wait_ge(s_xn, GB * g + j + 1)
                    t = tokens(g)[:, j, :]
                    pool.tensor_tensor(t, t, s1_bc, ALU.mult).then_inc(s_sc, 1)

            def high(g):
                for c in range(DC):
                    s = g * DC + c
                    pool.wait_ge(s_f, s + 1)
                    if s >= FR:
                        pool.wait_ge(s_parts[s % FR], 16 * (s // FR))
                    pool.tensor_copy(ring_hl[:, s % FR, 0, :], ring_f[:, s % FR, :]).then_inc(s_hi, 1)

            def convert(b, k, parts, s, count, b_count):
                a = mask[:, b, :, :].rearrange("p a n -> p (a n)")
                w = 2 * N // parts
                a = a[:, k * w:(k + 1) * w]
                pool.wait_ge(s, count)
                pool.nop(nofuse=True)
                pool.tensor_scalar(a, a.bitcast(I32), 0.0, NEG, ALU.is_equal, ALU.mult).then_inc(s_m, 1)

            for g in range(2 * NG + 2):
                if g < NG:
                    norm_x(g)
                if 0 <= g - 1 < 2 * NG:
                    norm(g - 1)
                    scale(g - 1)
                if 0 <= g - 2:
                    high(g - 2)
                if g == NG:
                    for k in range(4):
                        convert(0, k, 4, s_adj0, 16, 0)
            pool.wait_ge(s_parts[FR - 1], 16 * (2 * NG * DC // FR))
            for k in range(4):
                convert(1, k, 4, s_adj1, 16, 0)

            PIECES = 16

            def body(i, last):
                for t in range(BCH // 2):
                    p, j = t // (PCH // 2), t % (PCH // 2)
                    pp = (p - 1) % 2
                    fresh = not ((isinstance(i, int) and i == 0 and p == 0) or (last and p == 1))
                    pool.wait_ge(s_mx, i * BCH + 2 * t + 2)
                    if t >= MR // 2 or not (isinstance(i, int) and i == 0):
                        pool.wait_ge(s_exp, i * BCH + 2 * t - MR + 2)
                    pool.nop(nofuse=True)
                    pool.tensor_scalar(minrow[:, t % (MR // 2):t % (MR // 2) + 1],
                                       minhalf[:, 2 * t % MR:2 * t % MR + 1],
                                       minhalf[:, (2 * t + 1) % MR:(2 * t + 1) % MR + 1], None,
                                       ALU.min).then_inc(s_nm, 1)
                    if fresh and 5 <= j < 5 + PIECES // 2:
                        load = 16 * (i + 2) if p == 1 else 16 * (i + 1)
                        for k in (2 * (j - 5), 2 * (j - 5) + 1):
                            convert(pp, k, PIECES, (s_adj0, s_adj1)[pp], load, 0)

            body(0, False)
            with pool.Fori(1, TRIPS - 1) as i:
                body(i, False)
            body(TRIPS - 1, True)

            def add_parts(g):
                pool.wait_ge(s_cin[g % 2], 16 * DC * HG * (g // 2 + 1))
                for c in range(DC):
                    a = cin[:, g % 2, c, :, :]
                    pool.tensor_tensor(a[:, 0, :], a[:, 0, :], a[:, 1, :], ALU.add).then_inc(s_add, 1)

            def norm3(g):
                b = g % 2
                pool.wait_ge(s_mv3, GB * (g + 1))
                small3(pool.tensor_scalar(vareps[:, b, :], mv[:, b, :, 1], EPS, None, ALU.add))
                if g >= 2:
                    pool.wait_ge(s_n2, GB * (g - 1))
                pool.tensor_tensor(rstd[:, b, :], vareps[:, b, :], half_neg[:], ALU.pow).then_inc(s_r3, 1)

            step3 = [0]

            def small3(ins):
                step3[0] += 1
                ins.then_inc(s_p3, 1)
                pool.wait_ge(s_p3, step3[0])

            def add_x(g):
                for j in range(GB):
                    pool.wait_ge(s_y1, GB * g + j + 1)
                    pool.wait_ge(s_xr, 16 * (g + 1))
                    pool.tensor_tensor(xres[:, j, :], xres[:, j, :], ht2[:, g % 2 * GB + j, :], ALU.add).then_inc(s_y2, 1)

            add_parts(0)
            norm3(0)
            for g in range(NG):
                if g + 1 < NG:
                    add_parts(g + 1)
                    norm3(g + 1)
                add_x(g)

        @block.scalar
        def _(act):
            def relu(g):
                b = g % 2
                act.wait_ge(s_r1, g + 1)
                for j in range(GB):
                    t = tokens(g)[:, j, :]
                    act.activation(t, t, ACT.Relu, bias=nbias1[:, b, j:j + 1],
                                   scale=rstd1[:, b, j:j + 1]).then_inc(s_relu, 1)

            def normalise(g):
                b = g % 2
                act.wait_ge(s_r2, g + 1)
                for j in range(GB):
                    t = tokens(g)[:, j, :]
                    act.activation(t, t, ACT.Identity, bias=nbias[:, b, j:j + 1],
                                   scale=rstd[:, b, j:j + 1]).then_inc(s_xn, 1)

            def copy_turned(g):
                act.wait_ge(s_tp, DC * g + 2)
                act.activation(turned(g)[:, 1, :], bank[1], ACT.Copy).then_inc(s_tcA, 1)

            def copy_projected(g):
                for c in range(DC):
                    s = g * DC + c
                    act.wait_ge(s_prj, s + 1)
                    if s >= FR:
                        act.wait_ge(s_lo, s - FR + 1)
                    keys = g < NG
                    if s == 0:
                        act.wait_ge(s_const, 5)
                    act.activation(ring_f[:, s % FR, :], bank[2 + s % 2], ACT.Identity,
                                   bias=(kbias if keys else qbias_s)[:, c:c + 1],
                                   scale=1.0 if keys else QSCALE).then_inc(s_f, 1)

            for g in range(2 * NG + 2):
                if g < NG:
                    relu(g)
                if 0 <= g - 1 < 2 * NG:
                    normalise(g - 1)
                if 0 <= g - 2:
                    copy_turned(g - 2)
                    copy_projected(g - 2)

            def exps(i, m):
                t, half = m // 2, m % 2
                p, c, h = m // PCH, (m % UCH) // 2, m // UCH % H
                wait(act, s_nm, i * (BCH // 2) + t + 1)
                wait(act, s_mx, i * BCH + 2 * t + 2)
                a = prob[:, t % PR, half * CH:(half + 1) * CH]
                if m % PCH == 0:
                    wait(act, s_den, i * PAIRS_IN_BODY + p - 1)
                act.activation(a, a, ACT.Exp, bias=minrow[:, t % (MR // 2):t % (MR // 2) + 1], scale=-1.0,
                               accum_out=denhalf[:, p % 2, half, c, h:h + 1]).then_inc(s_exp, 1)

            def copy_b(i, m):
                u, c, half = m // UCH, (m % UCH) // 2, m % 2
                wait(act, s_trB, i * BCH + m + 1)
                if m % UCH == 0:
                    wait(act, s_pv, i * BU + u - 1)
                act.activation(
                    probT[:, u % 2, half * 8 + 4:half * 8 + 8, c * P:(c + 1) * P],
                    trB[:].rearrange("p (s t) -> p s t", t=P), ACT.Copy).then_inc(s_evB, 1)

            def slice_(i, n, first, over):
                if not (first and n < EXP_LAG) and not (over and n >= EXP_LAG):
                    exps(i, n - EXP_LAG)
                if not (first and n < T_LAG) and not (over and n >= T_LAG):
                    copy_b(i, n - T_LAG)

            for n in range(BCH):
                slice_(0, n, True, False)
            with act.Fori(1, TRIPS) as i:
                for n in range(BCH):
                    slice_(i, n, False, False)
            for n in range(T_LAG):
                slice_(TRIPS, n, False, True)

            def front(g):
                act.wait_ge(s_rt, g + 1)
                if g >= 1:
                    act.wait_ge(s_rb, g * DC)
                act.activation(rdT[:], bank[0][0:H, :], ACT.Copy).then_inc(s_rtc, 1)

            def mask3(g):
                for j in range(GB):
                    act.wait_ge(s_n2, GB * g + j + 1)
                    if g >= 2:
                        act.wait_ge(s_y2, GB * (g - 1))
                    act.activation(ht2[:, g % 2 * GB + j, :], hid[:, j, :], ACT.Copy,
                                   scale=nmaskf[:, g * GB + j:g * GB + j + 1]).then_inc(s_n3, 1)

            def copy3(g):
                for c in range(DC):
                    act.wait_ge(s_t3, DC * g + c + 1)
                    if g >= 1:
                        act.wait_ge(s_f1, FC * g)
                    act.activation(hidT[:, c, :], bank[2 + c], ACT.Copy).then_inc(s_c3, 1)

            def gelu(g):
                for f in range(FC):
                    act.wait_ge(s_f1, FC * g + f + 1)
                    if g >= 2:
                        act.wait_ge(s_f2, GB * (g - 1))
                    act.activation(gel[:, g % 2, f, :], bank[4 + f % 2], ACT.Gelu_apprx_tanh).then_inc(s_g, 1)

            for r in range(CR):
                act.wait_ge(s_cst[r], 16 * (NPAIR * H // CR))
            front(0)
            mask3(0)
            copy3(0)
            for g in range(NG):
                if g + 1 < NG:
                    front(g + 1)
                gelu(g)
                if g + 1 < NG:
                    mask3(g + 1)
                    copy3(g + 1)

        @block.vector
        def _(dve):
            def moments(g, src_stats, dst, s_out_):
                b = g % 2
                for j in range(GB):
                    dve.bn_stats(src_stats[:, j, :], tokens(g)[:, j, :]).then_inc(s_stat, 1)
                count[0] += GB
                dve.wait_ge(s_stat, count[0])
                for j in range(GB):
                    dve.bn_aggr(dst[:, b, j, :], src_stats[:, j, :]).then_inc(s_out_, 1)

            count = [0]

            def moments_x(g):
                dve.wait_ge(s_xin[g], 16)
                if g >= 1:
                    dve.wait_ge(s_mv1, GB * g)
                if g >= 2:
                    dve.wait_ge(s_r1, g - 1)
                moments(g, stats, mv, s_mv1)

            def moments_h(g):
                if g < NG:
                    dve.wait_ge(s_relu, GB * (g + 1))
                else:
                    dve.wait_ge(s_xin[g], 16)
                if g >= 1:
                    dve.wait_ge(s_mv2, GB * g)
                if g >= 2:
                    dve.wait_ge(s_r2, g - 1)
                moments(g, stats2, mv2, s_mv2)

            def shift(g):
                k = g % NG
                for j in range(GB):
                    dve.wait_ge(s_sc, GB * g + j + 1)
                    if g == 0 and j == 0:
                        dve.wait_ge(s_const, 5)
                    t = tokens(g)[:, j, :]
                    dve.scalar_tensor_tensor(t, b1_bc, nmaskf[:, k * GB + j:k * GB + j + 1], t,
                                             ALU.mult, ALU.add).then_inc(s_ln, 1)

            def copy_turned(g):
                dve.wait_ge(s_tp, DC * g + 1)
                dve.tensor_copy(turned(g)[:, 0, :], bank[0]).then_inc(s_tcD, 1)

            def low(g):
                for c in range(DC):
                    s = g * DC + c
                    dve.wait_ge(s_hi, s + 1)
                    dve.tensor_tensor(ring_hl[:, s % FR, 1, :], ring_f[:, s % FR, :],
                                      ring_hl[:, s % FR, 0, :].bitcast(F32), ALU.subtract).then_inc(s_lo, 1)

            def copy_values(g):
                for j in range(GB):
                    dve.wait_ge(s_vp, GB * g + j + 1)
                    dve.tensor_tensor(vals[:, g * GB + j, :], bank[4 + j % 4][:, 0:D], bv_bc,
                                      ALU.add).then_inc(s_ve, 1)

            for g in range(2 * NG + 2):
                if g < NG:
                    moments_x(g)
                if 0 <= g - 1 < 2 * NG:
                    moments_h(g - 1)
                    shift(g - 1)
                if 0 <= g - 2:
                    copy_turned(g - 2)
                    if g - 2 < NG:
                        copy_values(g - 2)
                    low(g - 2)

            def copy_a(i, m):
                u, c, half = m // UCH, (m % UCH) // 2, m % 2
                if m % UCH == 0:
                    wait(dve, s_pv, i * BU + u - 1)
                wait(dve, s_trA, i * BCH + m + 1)
                dve.tensor_copy(
                    probT[:, u % 2, half * 8:half * 8 + 4, c * P:(c + 1) * P],
                    trA[:].rearrange("p (s t) -> p s t", t=P)).then_inc(s_evA, 1)

            def masked_min(i, n):
                t, half = n // 2, n % 2
                p, c = n // PCH, (n % UCH) // 2
                dve.tensor_tensor_reduce(
                    out=prob[:, t % PR, half * CH:(half + 1) * CH], in0=score[n % 2][:],
                    in1=mask[:, p % 2, c, half * CH:(half + 1) * CH], scale=1.0, scalar=HUGE,
                    op0=ALU.add, op1=ALU.min, accum_out=minhalf[:, n % MR:n % MR + 1]).then_inc(s_mx, 1)

            def copy_context(i, u):
                wait(dve, s_pv, i * BU + u + 1)
                if not (isinstance(i, int) and i == 0 and u < CR):
                    dve.wait_ge(s_cst[u % CR], 16 * (i * (BU // CR) + u // CR))
                dve.tensor_copy(cpart[:, u % CR, :], pv[u % 2][:, 0:PAIR]).then_inc(s_ctx, 1)

            def denominators(i, p):
                pair = i * PAIRS_IN_BODY + p
                wait(dve, s_exp, pair * PCH + PCH)
                d = denhalf[:, p % 2, :, :, :].rearrange("p a b h -> p a (b h)")
                o = den[:].rearrange("p b h -> p (b h)")[:, bass.ds(pair * 2 * H, 2 * H)]
                dve.tensor_tensor(o, d[:, 0, :], d[:, 1, :], ALU.add).then_inc(s_den, 1)

            def slice_(i, n, first, over):
                if n % UCH == 0 and not (first and n < CTX_LAG + 1) and not (over and n >= CTX_LAG + 1):
                    copy_context(i, (n - CTX_LAG - 1) // UCH)
                if n % PCH == 6 and not (first and n < PCH) and not (over and n >= PCH):
                    denominators(i, n // PCH - 1)
                if not over and n % PCH == 0:
                    if first:
                        dve.wait_ge(s_m, 4 * (n // PCH + 1))
                    else:
                        dve.wait_ge(s_m, 8 + 16 * (i * PAIRS_IN_BODY + n // PCH - 1))
                if not (first and n < T_LAG) and not (over and n >= T_LAG):
                    copy_a(i, n - T_LAG)
                if not over:
                    if first:
                        dve.wait_ge(s_qk, n + 1)
                    masked_min(i, n)

            dve.wait_ge(s_hts, 16 * NG)
            for n in range(BCH):
                slice_(0, n, True, False)
            with dve.Fori(1, TRIPS) as i:
                for n in range(BCH):
                    slice_(i, n, False, False)
            for n in range(CTX_LAG + 2):
                slice_(TRIPS, n, False, True)

            dve.wait_ge(s_den, NPAIR)
            dve.reciprocal(rden[:], den[:]).then_inc(s_rd, 1)

            def front(g):
                dve.wait_ge(s_cin[g % 2], 16 * DC * HG * (g // 2 + 1))
                for c in range(DC):
                    a = cin[:, g % 2, c, :, :]
                    dve.tensor_tensor(a[:, 2, :], a[:, 2, :], a[:, 3, :], ALU.add).then_inc(s_add2, 1)
                for c in range(DC):
                    a = cin[:, g % 2, c, :, :]
                    dve.wait_ge(s_add, DC * g + c + 1)
                    dve.wait_ge(s_add2, 2 * DC * g + c + 1)
                    dve.tensor_tensor(a[:, 0, :], a[:, 0, :], a[:, 2, :], ALU.add).then_inc(s_add2, 1)
                for c in range(DC):
                    a = cin[:, g % 2, c, :, :]
                    dve.wait_ge(s_rb, DC * g + c + 1)
                    dve.wait_ge(s_add2, 2 * DC * g + DC + c + 1)
                    if g >= 1:
                        dve.wait_ge(s_wo, GB * g)
                    dve.tensor_tensor(cnorm[:, c, :], bank[2 + c], a[:, 0, :], ALU.mult).then_inc(s_cn, 1)

            def middle(g):
                for j in range(GB):
                    dve.wait_ge(s_wo, GB * g + 2 * (j // 2) + 2)
                    if g == 0 and j == 0:
                        dve.wait_ge(s_w3, 16 * 6)
                    if g >= 1:
                        dve.wait_ge(s_n3, GB * g)
                    dve.tensor_tensor(hid[:, j, :], bank[j // 2][:, D * (j % 2):D * (j % 2) + D], bo_bc,
                                      ALU.add).then_inc(s_h1, 1)
                for j in range(GB):
                    dve.wait_ge(s_h1, GB * g + j + 1)
                    tb = g * GB + j
                    dve.wait_ge(s_htin, 16 * (g + 1))
                    dve.scalar_tensor_tensor(hid[:, j, :], hid[:, j, :], nmaskf[:, tb:tb + 1], htin[:, j, :],
                                             ALU.mult, ALU.add).then_inc(s_h2, 1)
                back(g - 1, 0)
                b = g % 2
                for j in range(GB):
                    dve.wait_ge(s_h2, GB * g + j + 1)
                    if g >= 1:
                        dve.wait_ge(s_mv3, GB * g)
                    dve.bn_stats(stats[:, j, :], hid[:, j, :]).then_inc(s_st3, 1)
                for j in range(GB):
                    dve.wait_ge(s_st3, GB * g + j + 1)
                    dve.bn_aggr(mv[:, b, j, :], stats[:, j, :]).then_inc(s_mv3, 1)
                back(g - 1, 1)
                dve.wait_ge(s_mv3, GB * (g + 1))
                for j in range(GB):
                    dve.scalar_tensor_tensor(hid[:, j, :], hid[:, j, :], mv[:, b, j, 0:1], s2_bc,
                                             ALU.subtract, ALU.mult).then_inc(s_n1, 1)
                back(g - 1, 2)
                dve.wait_ge(s_r3, g + 1)
                for j in range(GB):
                    dve.wait_ge(s_n1, GB * g + j + 1)
                    dve.scalar_tensor_tensor(hid[:, j, :], hid[:, j, :], rstd[:, b, j:j + 1], b2_bc,
                                             ALU.mult, ALU.add).then_inc(s_n2, 1)

                back(g - 1, 3)

            def back(g, j):
                if g >= 0:
                    dve.wait_ge(s_f2, GB * g + j + 1)
                    r = ht2[:, g % 2 * GB + j, :]
                    dve.tensor_tensor(r, bank[6 + j % 2][:, 0:D], r, ALU.add).then_inc(s_y1, 1)

            for g in range(NG):
                front(g)
                middle(g)
            for j in range(GB):
                back(NG - 1, j)

        @block.tensor
        def _(pe):
            def turn(g):
                if g == 0:
                    pe.wait_ge(s_const, 5)
                for c in range(DC):
                    for j in range(GB):
                        if c == 0:
                            pe.wait_ge(s_ln, GB * g + j + 1)
                        if j == 0 and g >= 1:
                            pe.wait_ge((s_tcD, s_tcA)[c], g)
                        mm = pe.transpose(bank[c][:, j * P:(j + 1) * P], tokens(g)[:, j, c * P:(c + 1) * P],
                                          ident[:])
                    mm.then_inc(s_tp, 1)

            def project(g):
                w = wqkv[:, 1 if g < NG else 0, :, :]
                pe.wait_ge(s_tcD, g + 1)
                pe.wait_ge(s_tcA, g + 1)
                for m in range(DC):
                    s = g * DC + m
                    if s >= 2:
                        pe.wait_ge(s_f, s - 1)
                    for c in range(DC):
                        mm = pe.matmul(bank[2 + s % 2], w[:, c, m * P:(m + 1) * P], turned(g)[:, c, :],
                                       start=(c == 0), stop=(c == DC - 1))
                    mm.then_inc(s_prj, 1)

            def project_values(g):
                for j in range(GB):
                    if g >= 1:
                        pe.wait_ge(s_ve, GB * (g - 1) + j + 1)
                    for c in range(DC):
                        mm = pe.matmul(bank[4 + j % 4][:, 0:D], turned(g)[:, c, j * P:(j + 1) * P],
                                       wqkv[:, 2, c, :], start=(c == 0), stop=(c == DC - 1))
                    mm.then_inc(s_vp, 1)

            for g in range(2 * NG):
                turn(g)
                project(g)
                if g < NG:
                    project_values(g)

            def scores(i, n):
                p, h, c, half = n // PCH, n // UCH % H, (n % UCH) // 2, n % 2
                wait(pe, s_mx, i * BCH + n - 1)
                for k in range(CH // GT):
                    at = half * CH + k * GT
                    mm = pe.matmul(score[n % 2][:, k * GT:(k + 1) * GT],
                                   qst[:, p % 2, h, c * P:(c + 1) * P], kst[:, h, at:at + GT],
                                   start=True, stop=True)
                mm.then_inc(s_qk, 1)

            def turn_probs(i, m):
                t, half = m // 2, m % 2
                wait(pe, s_exp, i * BCH + m + 1)
                for dst, s_free, s_done, b0 in ((trA, s_evA, s_trA, 0), (trB, s_evB, s_trB, 4)):
                    wait(pe, s_free, i * BCH + m)
                    for b in range(4):
                        at = (half * 8 + b0 + b) * P
                        mm = pe.transpose(dst[:, b * P:(b + 1) * P], prob[:, t % PR, at:at + P], ident[:])
                    mm.then_inc(s_done, 1)

            def context(i, u, k):
                h = u % H
                if k == 0:
                    wait(pe, s_evA, i * BCH + UCH * u + UCH)
                    wait(pe, s_evB, i * BCH + UCH * u + UCH)
                    wait(pe, s_ctx, i * BU + u - 1)
                for j in range(HG):
                    sblk = HG * k + j
                    mm = pe.matmul(pv[u % 2][HD * j:HD * (j + 1), 0:PAIR], vals[:, sblk, h * HD:(h + 1) * HD],
                                   probT[:, u % 2, sblk, :], start=(k == 0), stop=(k == NB // HG - 1))
                if k == NB // HG - 1:
                    mm.then_inc(s_pv, 1)

            def slice_(i, n, first, over):
                if not over:
                    if n % PCH == 0:
                        pe.wait_ge(s_qst[n // PCH], 64 * (i + 1))
                    if first and n in (0, UCH, 2 * UCH, 4 * UCH):
                        k = (0, UCH, 2 * UCH, 4 * UCH).index(n)
                        pe.wait_ge(s_kst[k], 64)
                    scores(i, n)
                if not (first and n < T_LAG) and not (over and n >= T_LAG):
                    turn_probs(i, n - T_LAG)
                if not (first and n < PV_LAG) and not (over and n >= PV_LAG + UCH):
                    m = n - PV_LAG
                    if not over or m < 0:
                        context(i, m // UCH, m % UCH)

            pe.wait_ge(s_lo, 2 * NG * DC)
            pe.wait_ge(s_ve, GB * NG)
            for n in range(BCH):
                slice_(0, n, True, False)
            with pe.Fori(1, TRIPS) as i:
                for n in range(BCH):
                    slice_(i, n, False, False)
            for n in range(PV_LAG):
                slice_(TRIPS, n, False, True)

            pe.wait_ge(s_mx, NPAIR * PCH)
            pe.wait_ge(s_evA, NPAIR * PCH)
            pe.wait_ge(s_evB, NPAIR * PCH)
            pe.wait_ge(s_ctx, NPAIR * H)

            def front(g):
                pe.wait_ge(s_rd, 1)
                if g >= 1:
                    pe.wait_ge(s_h1, GB * g)
                for j in range(GB):
                    mm = pe.transpose(bank[0][0:H, j * P:(j + 1) * P], rden[:, g * GB + j, :], ident[:])
                mm.then_inc(s_rt, 1)
                pe.wait_ge(s_rtc, g + 1)
                if g >= 1:
                    pe.wait_ge(s_c3, DC * g)
                for c in range(DC):
                    pe.matmul(bank[2 + c], head_sel[:, c * P:(c + 1) * P], rdT[:],
                              start=True, stop=True).then_inc(s_rb, 1)

            def project_out(g):
                pe.wait_ge(s_cn, DC * (g + 1))
                for j in range(GB):
                    for c in range(DC):
                        mm = pe.matmul(bank[j // 2][:, D * (j % 2):D * (j % 2) + D],
                                       cnorm[:, c, j * P:(j + 1) * P], wo[:, c, :],
                                       start=(c == 0), stop=(c == DC - 1))
                    mm.then_inc(s_wo, 1)

            def turn3(g):
                for c in range(DC):
                    for j in range(GB):
                        if c == 0:
                            pe.wait_ge(s_n3, GB * g + j + 1)
                        if g >= 1 and j == 0:
                            pe.wait_ge(s_c3, DC * (g - 1) + c + 1)
                        mm = pe.transpose(bank[2 + c][:, j * P:(j + 1) * P],
                                          ht2[:, g % 2 * GB + j, c * P:(c + 1) * P], ident[:])
                    mm.then_inc(s_t3, 1)

            def ffn1(g):
                pe.wait_ge(s_c3, DC * (g + 1))
                if g == 0:
                    pe.wait_ge(s_w3, 16 * 6)
                for f in range(FC):
                    if g * FC + f >= 2:
                        pe.wait_ge(s_g, g * FC + f - 1)
                    for c in range(DC):
                        mm = pe.matmul(bank[4 + f % 2], w1[:, c, f * P:(f + 1) * P], hidT[:, c, :],
                                       start=(c == 0), stop=(c == DC - 1))
                    mm.then_inc(s_f1, 1)

            def ffn2(g):
                pe.wait_ge(s_g, FC * (g + 1))
                for j in range(GB):
                    if GB * g + j >= 2:
                        pe.wait_ge(s_y1, GB * g + j - 1)
                    for f in range(FC):
                        mm = pe.matmul(bank[6 + j % 2][:, 0:D], gel[:, g % 2, f, j * P:(j + 1) * P],
                                       w2[:, f, :], start=(f == 0), stop=(f == FC - 1))
                    mm.then_inc(s_f2, 1)

            front(0)
            project_out(0)
            turn3(0)
            for g in range(NG):
                if g + 1 < NG:
                    front(g + 1)
                ffn1(g)
                if g + 1 < NG:
                    project_out(g + 1)
                ffn2(g)
                if g + 1 < NG:
                    turn3(g + 1)


_INS = ["x", "adj", "nodemask", "L0_gnn_h_target", "L0_gnn_ln1_scale", "L0_gnn_ln1_bias",
        "L0_gnn_Wq", "L0_gnn_bq", "L0_gnn_Wk", "L0_gnn_bk", "L0_gnn_Wv", "L0_gnn_bv", "L0_gnn_Wo",
        "L0_gnn_bo", "L0_gnn_ln2_scale", "L0_gnn_ln2_bias", "L0_gnn_W1", "L0_gnn_W2"]


def kernel(**inputs):
    import numpy as np
    import concourse.bacc as bacc
    from concourse.bass_utils import run_bass_kernel_spmd

    nc = bacc.Bacc("TRN2", target_bir_lowering=False, num_devices=1)
    arrays, args = {}, []
    for name in _INS:
        a = np.ascontiguousarray(inputs[name])
        arrays[f"in_{name}"] = a
        args.append(nc.dram_tensor(f"in_{name}", a.shape, mybir.dt.from_np(a.dtype), kind="ExternalInput").ap())
    out = nc.dram_tensor("out_0", (N, D), F32, kind="ExternalOutput").ap()
    program(nc, *args, out)
    r = run_bass_kernel_spmd(nc, [arrays], core_ids=[0])
    return r.results[0]["out_0"]
```

```python
from contextlib import ExitStack

import concourse.bass as bass
from concourse import mybir

ALU = mybir.AluOpType
ACT = mybir.ActivationFunctionType
AX = mybir.AxisListType
F32 = mybir.dt.float32
F32R = mybir.dt.float32r
I32 = mybir.dt.int32

P = 128
N = 2048
D = 256
H = 8
HD = D // H
F = 4 * D
EPS = 1e-5
NEG = 1e30
HUGE = 3e38
QSCALE = -float(HD) ** -0.5

NB = N // P
DC = D // P
FC = F // P
GT = 512
GB = GT // P
NG = N // GT
HG = P // HD

PAIR = 2 * P
NPAIR = N // PAIR
CH = 1024
UCH = 2 * N // CH
PCH = UCH * H
PAIRS_IN_BODY = 2
BCH = PAIRS_IN_BODY * PCH
BU = PAIRS_IN_BODY * H
TRIPS = NPAIR // PAIRS_IN_BODY

EXP_LAG = 3
T_LAG = 4
PV_LAG = T_LAG + UCH
CTX_LAG = PV_LAG + UCH
SUM_LAG = CTX_LAG + UCH * (HG - 1) + 1
SUM_COPY_LAG = SUM_LAG + 1
DEN_AT = EXP_LAG + 4
SCH = UCH * HG

PR = 4
MR = 16
CR = HG
FR = 4


def program(nc, x, adj, nodemask, h_target, ln1_scale, ln1_bias, Wq, bq, Wk, bk, Wv, bv, Wo, bo,
            ln2_scale, ln2_bias, W1, W2, out):
    with ExitStack() as ctx:
        def sb(name, shape, dt=F32):
            return ctx.enter_context(nc.sbuf_tensor(name, shape, dt))

        def sem(name):
            return ctx.enter_context(nc.semaphore(name))

        parts_scr = nc.dram_tensor("parts_scr", (2, 2, D, N), F32).ap()
        ctx_scr = nc.dram_tensor("ctx_scr", (D, N), F32).ap()
        ht_scr = nc.dram_tensor("ht_scr", (N, D), F32).ap()

        kst = sb("kst", [P, H, N], F32R)
        qst = sb("qst", [P, 2, H, PAIR], F32R)
        vals = sb("vals", [P, NB, D])
        prob = sb("prob", [P, PR, N])
        probT = sb("probT", [P, 2, NB, PAIR])
        mask = sb("mask", [P, 2, 2, N])
        cpart = sb("cpart", [P, CR, PAIR])
        csum = sb("csum", [P, 2, PAIR])
        cin0 = sb("cin0", [P, DC, GT])
        ident = sb("ident", [P, P])
        part_sel = sb("part_sel", [P, HD])
        head_sel = sb("head_sel", [H, D])
        minhalf = sb("minhalf", [P, MR])
        minrow = sb("minrow", [P, MR // 2])
        denhalf = sb("denhalf", [P, 2, 2, 2, H])
        den = sb("den", [P, NB, H])
        rden = sb("rden", [P, NB, H])
        half_neg = sb("half_neg", [P, GB])
        nmask_i = sb("nmask_i", [NB, P], I32)
        nmask_r = sb("nmask_r", [NB, P])
        bias_r = sb("bias_r", [2 * DC, P])
        nmaskf = sb("nmaskf", [P, NB])
        kbias = sb("kbias", [P, DC])
        qbias_s = sb("qbias_s", [P, DC])
        stats = sb("stats", [P, GB, 6])
        stats2 = sb("stats2", [P, GB, 6])
        mv = sb("mv", [P, 2, GB, 2])
        mv2 = sb("mv2", [P, 2, GB, 2])
        vareps = sb("vareps", [P, 2, GB])
        rstd = sb("rstd", [P, 2, GB])
        rstd1 = sb("rstd1", [P, 2, GB])
        nbias = sb("nbias", [P, 2, GB])
        nbias1 = sb("nbias1", [P, 2, GB])
        tmpa = sb("tmpa", [P, GB])
        tmpb = sb("tmpb", [P, GB])
        tmpc = sb("tmpc", [P, GB])

        xs = prob[:, 0:2, :].rearrange("p a (b d) -> p (a b) d", d=D)
        turned_ring = prob[:, 2, :].rearrange("p (r c n) -> p r c n", r=2, c=DC)
        spare = probT[:, 1, :, :].rearrange("p b t -> p (b t)")
        ring_f = spare[:, 0:FR * GT].rearrange("p (r n) -> p r n", r=FR)
        ofs = FR * GT
        s1_bc = spare[:, ofs:ofs + D]
        b1_bc = spare[:, ofs + D:ofs + 2 * D]
        ofs += 2 * D
        wqkv = spare[:, ofs:ofs + 3 * DC * D].rearrange("p (w c n) -> p w c n", w=3, c=DC)
        cspare = cpart[:, :, :].rearrange("p r t -> p (r t)")
        bv_bc = cspare[:, 0:D]
        ring_hl = mask[:, 1, :, :].rearrange("p a n -> p (a n)").bitcast(F32R).rearrange(
            "p (r s n) -> p r s n", r=FR, s=2)

        w1 = mask[:, 0, 0, :].rearrange("p (c f) -> p c f", c=DC)
        w2 = mask[:, 0, 1, :].rearrange("p (c d) -> p c d", c=FC)
        gel = prob[:, :, :].rearrange("p (b a) (c n) -> p b (a c) n", b=2, n=GT)
        cin_rest = probT[:, :, :, :].rearrange("p b s t -> p (b s t)")[:, 0:(NG - 1) * DC * GT].rearrange(
            "p (g c n) -> p g c n", g=NG - 1, c=DC)
        m1 = mask[:, 1, :, :].rearrange("p a n -> p (a n)")
        s2_bc = m1[:, 0:D]
        b2_bc = m1[:, D:2 * D]
        bo_bc = m1[:, 2 * D:3 * D]
        hid = m1[:, 1024:2048].rearrange("p (b d) -> p b d", d=D)
        hidT = m1[:, 2048:3072].rearrange("p (c n) -> p c n", c=DC)
        xres = m1[:, 3072:4096].rearrange("p (b d) -> p b d", d=D)
        ht2 = vals[:, 0:2 * GB, :]
        htin = vals[:, 2 * GB:3 * GB, :]
        cnorm = vals[:, 3 * GB:4 * GB, :].rearrange("p b d -> p (b d)").rearrange("p (c n) -> p c n", c=DC)
        wo = cspare[:, 0:DC * D].rearrange("p (c n) -> p c n", c=DC)
        rdT = cspare[0:H, DC * D:DC * D + GT]

        score = [ctx.enter_context(nc.psum_tensor(f"score{i}", [P, CH], F32)) for i in range(2)]
        trA = ctx.enter_context(nc.psum_tensor("trA", [P, GT], F32))
        trB = ctx.enter_context(nc.psum_tensor("trB", [P, GT], F32))
        pv = ctx.enter_context(nc.psum_tensor("pv", [P, GT], F32))
        psum_sum = ctx.enter_context(nc.psum_tensor("psum_sum", [P, GT], F32))
        bank = [score[0][:, 0:GT], score[0][:, GT:CH], score[1][:, 0:GT], score[1][:, GT:CH],
                trA[:, :], trB[:, :], pv[:, :], psum_sum[:, :]]

        s_rows = sem("mask_and_biases_loaded")
        s_w1 = sem("ln1_loaded")
        s_w = sem("weights_loaded")
        s_ident = sem("identity_ready")
        s_rowsf = sem("mask_as_float")
        s_rowsT = sem("mask_and_biases_turned")
        s_xin = [sem(f"group_loaded{g}") for g in range(2 * NG)]
        s_adj0 = sem("adj_loaded0")
        s_adj1 = sem("adj_loaded1")
        s_psel = sem("part_selector_ready")
        s_biases = sem("biases_copied")
        s_zero = sem("constants_zeroed")
        s_const = sem("constants_ready")
        s_stat = sem("stats_taken")
        s_mv1 = sem("moments_x")
        s_mv2 = sem("moments")
        s_pc = sem("pool_small_step")
        s_r1 = sem("rstd_x_ready")
        s_r2 = sem("rstd_ready")
        s_relu = sem("relu_done")
        s_xn = sem("normalised")
        s_sc = sem("scaled")
        s_ln = sem("ln1_done")
        s_tp = sem("rows_transposed")
        s_tcD = sem("transposes_copied_vector")
        s_tcA = sem("transposes_copied_scalar")
        s_prj = sem("projected")
        s_vp = sem("values_projected")
        s_f = sem("projection_copied")
        s_hi = sem("high_part")
        s_lo = sem("low_part")
        s_ve = sem("values_copied")
        s_parts = [sem(f"parts_stored{r}") for r in range(FR)]
        s_kst = [sem(f"keys_stacked{h}") for h in range(4)]
        s_qst = [sem(f"queries_stacked{b}") for b in range(2)]
        s_hts = sem("targets_stored")
        s_htin = sem("targets_loaded")
        s_m0 = sem("first_mask_ready")
        s_m = sem("mask_ready")
        s_qk = sem("scores_ready")
        s_mx = sem("minimum_taken")
        s_nm = sem("minimum_of_row")
        s_exp = sem("exp_done")
        s_trA = sem("transposed_a")
        s_trB = sem("transposed_b")
        s_evA = sem("copied_a")
        s_evB = sem("copied_b")
        s_pv = sem("context_summed")
        s_ctx = sem("context_copied")
        s_sum = sem("parts_summed")
        s_sumc = sem("sums_copied")
        s_cst = [sem(f"context_stored{r}") for r in range(2)]
        s_den = sem("denominators")
        s_wol = sem("output_weights_loaded")
        s_w3 = sem("ffn_weights_loaded")
        s_cin = [sem(f"context_loaded{g}") for g in range(NG)]
        s_xr = sem("x_loaded")
        s_rd = sem("reciprocals")
        s_rt = sem("reciprocals_transposed")
        s_rtc = sem("reciprocals_copied")
        s_rb = sem("reciprocals_spread")
        s_cn = sem("context_normalised")
        s_wo = sem("output_projected")
        s_h1 = sem("bias_added")
        s_h2 = sem("residual_added")
        s_st3 = sem("stats_taken3")
        s_mv3 = sem("moments3")
        s_p3 = sem("pool_small_step3")
        s_r3 = sem("rstd3_ready")
        s_n1 = sem("centred3")
        s_n2 = sem("ln2_affine")
        s_n3 = sem("ln2_masked")
        s_t3 = sem("ln2_transposed")
        s_c3 = sem("ln2_copied")
        s_f1 = sem("ffn1_done")
        s_g = sem("gelu_done")
        s_f2 = sem("ffn2_done")
        s_y1 = sem("ffn_added")
        s_y2 = sem("x_added")
        s_out = sem("out_stored")

        def rows(a, g):
            return a.rearrange("(b p) d -> p b d", p=P)[:, g * GB:(g + 1) * GB, :]

        def wait(eng, s, value):
            if isinstance(value, int) and value <= 0:
                return
            eng.wait_ge(s, value)

        block = ctx.enter_context(nc.Block())

        STEPS = [("t", 0)] + [("s", g) for g in range(NG)] + [("t", g) for g in range(1, NG)]
        SLOTS = NG
        SOURCES = [k for k, (kind, _) in enumerate(STEPS) if kind == "s"]
        LAST_SOURCE = SOURCES[-1]

        def is_source(k):
            return STEPS[k][0] == "s"

        def sources_until(k):
            return sum(1 for j in SOURCES if j <= k)

        def targets_until(k):
            return k + 1 - sources_until(k)

        def tokens(k):
            return xs[:, k % SLOTS * GB:(k % SLOTS + 1) * GB, :]

        def turned(k):
            return turned_ring[:, k % 2, :, :]

        def slot_uses(r, s):
            return len([q for q in range(s) if q % FR == r])

        QUADRANTS = {1: (0, 1, 0, 1), 0: (0, 0, 1, 1)}
        KHEADS = [(0, 1), (1, 2), (2, 4), (4, 8)]

        def load_adj(sp, pair, s):
            b = 0 if s is s_adj0 else 1
            sp.dma_start(
                mask[:, b, :, :].bitcast(I32),
                adj[bass.ds(pair * PAIR, PAIR), :].rearrange("(b p) n -> p b n", p=P)).then_inc(s, 16)

        def load_queries(sp, pair, b):
            for quad in range(4):
                sp.dma_start(
                    qst[HD * quad:HD * (quad + 1), b, :, :].bitcast(F32),
                    parts_scr[0, QUADRANTS[0][quad], :, bass.ds(pair * PAIR, PAIR)].rearrange(
                        "(h d) n -> d h n", d=HD)).then_inc(s_qst[b], 16)

        @block.sync
        def _(sp):
            def load_rows(k):
                kind, g = STEPS[k]
                sp.dma_start(tokens(k), rows(x if kind == "s" else h_target, g)).then_inc(s_xin[k], 16)

            load_rows(0)
            load_rows(1)
            sp.dma_start(nmask_i[:], nodemask.rearrange("(b p) -> b p", p=P)).then_inc(s_rows, 16)
            sp.dma_start(bias_r[0:DC, :], bq.rearrange("(c p) -> c p", p=P)).then_inc(s_rows, 16)
            sp.dma_start(bias_r[DC:2 * DC, :], bk.rearrange("(c p) -> c p", p=P)).then_inc(s_rows, 16)
            sp.dma_start(s1_bc, ln1_scale.rearrange("(a d) -> a d", a=1).to_broadcast([P, D])).then_inc(s_w1, 16)
            sp.dma_start(b1_bc, ln1_bias.rearrange("(a d) -> a d", a=1).to_broadcast([P, D])).then_inc(s_w1, 16)
            load_rows(2)
            for j, w in enumerate((Wq, Wk, Wv)):
                sp.dma_start(wqkv[:, j, :, :], w.rearrange("(c p) n -> p c n", p=P)).then_inc(s_w, 16)
            sp.dma_start(bv_bc, bv.rearrange("(a d) -> a d", a=1).to_broadcast([P, D])).then_inc(s_w, 16)
            load_rows(3)
            load_adj(sp, 0, s_adj0)
            for s in range(len(STEPS) * DC):
                k, c = s // DC, s % DC
                kind, g = STEPS[k]
                which = 1 if kind == "s" else 0
                if c == 0:
                    if kind == "t":
                        sp.wait_ge(s_ln, GB * (k + 1))
                        sp.dma_start(rows(ht_scr, g), tokens(k)).then_inc(s_hts, 16)
                    if k + SLOTS < len(STEPS):
                        sp.wait_ge(s_tp, DC * (k + 1))
                        if kind == "t":
                            sp.wait_ge(s_hts, 16 * targets_until(k))
                        load_rows(k + SLOTS)
                sp.wait_ge(s_lo, s + 1)
                sp.wait_ge(s_hi, s + 1)
                sp.dma_start(
                    parts_scr[which, :, c * P:(c + 1) * P, g * GT:(g + 1) * GT].rearrange("s p n -> p s n"),
                    ring_hl[:, s % FR, :, :].bitcast(F32)).then_inc(s_parts[s % FR], 16)
                if s == LAST_SOURCE * DC + DC - 1:
                    for r in range(FR):
                        sp.wait_ge(s_parts[r], 16 * slot_uses(r, s + 1))
                    for n, (h0, h1) in enumerate(KHEADS):
                        for quad in range(4):
                            sp.dma_start(
                                kst[HD * quad:HD * (quad + 1), h0:h1, :].bitcast(F32),
                                parts_scr[1, QUADRANTS[1][quad], h0 * HD:h1 * HD, :].rearrange(
                                    "(h d) n -> d h n", d=HD)).then_inc(s_kst[n], 16)
                        if n < 2:
                            load_queries(sp, n, n)
            for r in range(FR):
                sp.wait_ge(s_parts[r], 16 * slot_uses(r, len(STEPS) * DC))
            load_adj(sp, 1, s_adj1)

            def store(i, v):
                p, c = v // DC, v % DC
                pair = i * PAIRS_IN_BODY + p
                sp.wait_ge(s_sumc, i * (BU // HG) + v + 1)
                sp.nop(nofuse=True)
                sp.dma_start(ctx_scr[c * P:(c + 1) * P, bass.ds(pair * PAIR, PAIR)],
                             csum[:, v % 2, :]).then_inc(s_cst[v % 2], 16)

            def refill(i, p):
                pair = i * PAIRS_IN_BODY + p
                sp.wait_ge(s_mx, pair * PCH + PCH)
                sp.nop(nofuse=True)
                load_adj(sp, pair + 2, (s_adj0, s_adj1)[p])
                sp.wait_ge(s_qk, pair * PCH + PCH)
                sp.nop(nofuse=True)
                load_queries(sp, pair + 2, p)

            def body(i, first, last):
                for p in range(PAIRS_IN_BODY):
                    if not (first and p == 0):
                        store(i, DC * p - 1)
                    store(i, DC * p)
                    if not last:
                        refill(i, p)

            body(0, True, False)
            with sp.Fori(1, TRIPS - 1) as i:
                body(i, False, False)
            body(TRIPS - 1, False, True)

            def load_context(g):
                sp.dma_start(cin0[:] if g == 0 else cin_rest[:, g - 1, :, :],
                             ctx_scr[:, g * GT:(g + 1) * GT].rearrange("(c p) n -> p c n", p=P)
                             ).then_inc(s_cin[g], 16)

            for r in range(2):
                sp.wait_ge(s_cst[r], 16 * (NPAIR * DC // 2 - 1))
            load_context(0)
            sp.wait_ge(s_mx, (NPAIR - 1) * PCH)
            sp.dma_start(w1, W1.rearrange("(c p) f -> p c f", p=P)).then_inc(s_w3, 16)
            sp.dma_start(w2, W2.rearrange("(c p) d -> p c d", p=P)).then_inc(s_w3, 16)
            sp.wait_ge(s_mx, NPAIR * PCH)
            for dst, src in ((s2_bc, ln2_scale), (b2_bc, ln2_bias), (bo_bc, bo)):
                sp.dma_start(dst, src.rearrange("(a d) -> a d", a=1).to_broadcast([P, D])).then_inc(s_w3, 16)
            store(TRIPS, -1)
            sp.wait_ge(s_sum, NPAIR * DC)
            sp.dma_start(wo, Wo.rearrange("(c p) n -> p c n", p=P)).then_inc(s_wol, 16)
            sp.dma_start(htin, rows(ht_scr, 0)).then_inc(s_htin, 16)
            for r in range(2):
                sp.wait_ge(s_cst[r], 16 * (NPAIR * DC // 2))
            for g in range(1, NG):
                load_context(g)
            for g in range(NG):
                if g >= 1:
                    sp.wait_ge(s_out, 16 * g)
                sp.dma_start(xres, rows(x, g)).then_inc(s_xr, 16)
                if g + 1 < NG:
                    sp.wait_ge(s_h2, GB * (g + 1))
                    sp.dma_start(htin, rows(ht_scr, g + 1)).then_inc(s_htin, 16)
                sp.wait_ge(s_y2, GB * (g + 1))
                sp.dma_start(rows(out, g), xres).then_inc(s_out, 16)
            sp.wait_ge(s_out, 16 * NG)

        @block.gpsimd
        def _(pool):
            pool.memset(ident[:], 0.0).then_inc(s_zero, 1)
            pool.memset(head_sel[:], 0.0).then_inc(s_zero, 1)
            pool.memset(half_neg[:], -0.5).then_inc(s_const, 1)
            pool.wait_ge(s_zero, 1)
            pool.affine_select(out=ident[:], in_=ident[:], compare_op=ALU.not_equal, fill=1.0, base=0,
                               pattern=[[-1, P]], channel_multiplier=1).then_inc(s_ident, 1)
            pool.wait_ge(s_rows, 16 * 3)
            pool.tensor_scalar(nmask_r[:], nmask_i[:], 1.0, None, ALU.is_equal).then_inc(s_rowsf, 1)
            pool.wait_ge(s_zero, 2)
            pool.affine_select(out=head_sel[:].rearrange("h (g d) -> h g d", d=HD),
                               in_=head_sel[:].rearrange("h (g d) -> h g d", d=HD),
                               compare_op=ALU.not_equal, fill=1.0, base=0,
                               pattern=[[-1, H], [0, HD]], channel_multiplier=1).then_inc(s_const, 1)
            pool.wait_ge(s_const, 1)

            PIECES = 16
            step = [0]

            def small(ins):
                step[0] += 1
                ins.then_inc(s_pc, 1)
                pool.wait_ge(s_pc, step[0])

            def root(var, b, dst):
                small(pool.tensor_scalar(vareps[:, b, :], var, EPS, None, ALU.add))
                small(pool.tensor_tensor(dst, vareps[:, b, :], half_neg[:], ALU.pow))

            def norm_x(k):
                b, n = k % 2, sources_until(k)
                pool.wait_ge(s_mv1, GB * n)
                if n > 2:
                    pool.wait_ge(s_relu, GB * (n - 2))
                root(mv[:, b, :, 1], b, rstd1[:, b, :])
                small(pool.tensor_tensor(tmpa[:], mv[:, b, :, 0], rstd1[:, b, :], ALU.mult))
                pool.tensor_scalar(nbias1[:, b, :], tmpa[:], -1.0, None, ALU.mult).then_inc(s_r1, 1)

            def norm(k):
                b, g = k % 2, STEPS[k][1]
                pool.wait_ge(s_mv2, GB * (k + 1))
                if k >= 2:
                    pool.wait_ge(s_xn, GB * (k - 1))
                if k == 0:
                    pool.wait_ge(s_rowsT, 2)
                root(mv2[:, b, :, 1], b, tmpb[:])
                small(pool.tensor_tensor(rstd[:, b, :], tmpb[:], nmaskf[:, g * GB:(g + 1) * GB], ALU.mult))
                small(pool.tensor_tensor(tmpc[:], mv2[:, b, :, 0], rstd[:, b, :], ALU.mult))
                pool.tensor_scalar(nbias[:, b, :], tmpc[:], -1.0, None, ALU.mult).then_inc(s_r2, 1)

            def scale(k):
                if k == 0:
                    pool.wait_ge(s_w1, 32)
                for j in range(GB):
                    pool.wait_ge(s_xn, GB * k + j + 1)
                    t = tokens(k)[:, j, :]
                    pool.tensor_tensor(t, t, s1_bc, ALU.mult).then_inc(s_sc, 1)

            def convert(b, k, s, count):
                w = 2 * N // PIECES
                a = mask[:, b, :, :].rearrange("p a n -> p (a n)")[:, k * w:(k + 1) * w]
                pool.wait_ge(s, count)
                pool.nop(nofuse=True)
                pool.tensor_scalar(a, a.bitcast(I32), 0.0, NEG, ALU.is_equal, ALU.mult).then_inc(s_m, 1)

            for st in range(len(STEPS) + 1):
                if 0 <= st - 1:
                    norm(st - 1)
                if st < len(STEPS) and is_source(st):
                    norm_x(st)
                if 0 <= st - 1:
                    scale(st - 1)

            def body(i, last):
                for t in range(BCH // 2):
                    p, j = t // (PCH // 2), t % (PCH // 2)
                    pp = (p - 1) % 2
                    fresh = not (last and p == 1)
                    pool.wait_ge(s_mx, i * BCH + 2 * t + 2)
                    if t >= MR // 2 or not (isinstance(i, int) and i == 0):
                        pool.wait_ge(s_exp, i * BCH + 2 * t - MR + 2)
                    pool.nop(nofuse=True)
                    pool.tensor_scalar(minrow[:, t % (MR // 2):t % (MR // 2) + 1],
                                       minhalf[:, 2 * t % MR:2 * t % MR + 1],
                                       minhalf[:, (2 * t + 1) % MR:(2 * t + 1) % MR + 1], None,
                                       ALU.min).then_inc(s_nm, 1)
                    if fresh and 5 <= j < 5 + PIECES // 2:
                        load = 16 * (i + 2) if p == 1 else 16 * (i + 1)
                        for k in (2 * (j - 5), 2 * (j - 5) + 1):
                            convert(pp, k, (s_adj0, s_adj1)[pp], load)

            body(0, False)
            with pool.Fori(1, TRIPS - 1) as i:
                body(i, False)
            body(TRIPS - 1, True)

            def norm3(g):
                b = g % 2
                pool.wait_ge(s_mv3, GB * (g + 1))
                small3(pool.tensor_scalar(vareps[:, b, :], mv[:, b, :, 1], EPS, None, ALU.add))
                if g >= 2:
                    pool.wait_ge(s_n2, GB * (g - 1))
                pool.tensor_tensor(rstd[:, b, :], vareps[:, b, :], half_neg[:], ALU.pow).then_inc(s_r3, 1)

            step3 = [0]

            def small3(ins):
                step3[0] += 1
                ins.then_inc(s_p3, 1)
                pool.wait_ge(s_p3, step3[0])

            def add_x(g):
                for j in range(GB):
                    pool.wait_ge(s_y1, GB * g + j + 1)
                    pool.wait_ge(s_xr, 16 * (g + 1))
                    pool.tensor_tensor(xres[:, j, :], xres[:, j, :], ht2[:, g % 2 * GB + j, :], ALU.add).then_inc(s_y2, 1)

            norm3(0)
            for g in range(NG):
                if g + 1 < NG:
                    norm3(g + 1)
                add_x(g)

        @block.scalar
        def _(act):
            act.wait_ge(s_rowsT, 1)
            act.activation(qbias_s[:], bank[7][:, NB:NB + DC], ACT.Copy, scale=QSCALE).then_inc(s_biases, 1)
            act.activation(kbias[:], bank[7][:, NB + DC:NB + 2 * DC], ACT.Copy).then_inc(s_biases, 1)

            def relu(k):
                b, n = k % 2, sources_until(k)
                act.wait_ge(s_r1, n)
                for j in range(GB):
                    t = tokens(k)[:, j, :]
                    act.activation(t, t, ACT.Relu, bias=nbias1[:, b, j:j + 1],
                                   scale=rstd1[:, b, j:j + 1]).then_inc(s_relu, 1)

            def normalise(k):
                b = k % 2
                act.wait_ge(s_r2, k + 1)
                for j in range(GB):
                    t = tokens(k)[:, j, :]
                    act.activation(t, t, ACT.Identity, bias=nbias[:, b, j:j + 1],
                                   scale=rstd[:, b, j:j + 1]).then_inc(s_xn, 1)

            def copy_turned(k):
                act.wait_ge(s_tp, DC * k + 2)
                if k >= 2:
                    act.wait_ge(s_prj, DC * (k - 1))
                    wait(act, s_vp, GB * sources_until(k - 2))
                act.activation(turned(k)[:, 1, :], bank[1], ACT.Copy).then_inc(s_tcA, 1)

            def copy_projected(k):
                for c in range(DC):
                    s = k * DC + c
                    act.wait_ge(s_prj, s + 1)
                    if s >= FR:
                        act.wait_ge(s_lo, s - FR + 1)
                    keys = is_source(k)
                    if s == 0:
                        act.wait_ge(s_biases, 2)
                    act.activation(ring_f[:, s % FR, :], bank[2 + s % 2], ACT.Identity,
                                   bias=(kbias if keys else qbias_s)[:, c:c + 1],
                                   scale=1.0 if keys else QSCALE).then_inc(s_f, 1)
                for c in range(DC):
                    s = k * DC + c
                    act.wait_ge(s_f, s + 1)
                    if s >= FR:
                        act.wait_ge(s_parts[s % FR], 16 * (s // FR))
                    act.activation(ring_hl[:, s % FR, 0, :], ring_f[:, s % FR, :],
                                   ACT.Copy).then_inc(s_hi, 1)

            for st in range(len(STEPS) + 4):
                if 0 <= st - 4:
                    copy_projected(st - 4)
                if 0 <= st - 3 < len(STEPS):
                    copy_turned(st - 3)
                if 0 <= st - 1 < len(STEPS):
                    normalise(st - 1)
                if st < len(STEPS) and is_source(st):
                    relu(st)

            def exps(i, m):
                t, half = m // 2, m % 2
                p, c, h = m // PCH, (m % UCH) // 2, m // UCH % H
                wait(act, s_nm, i * (BCH // 2) + t + 1)
                wait(act, s_mx, i * BCH + 2 * t + 2)
                a = prob[:, t % PR, half * CH:(half + 1) * CH]
                if m % PCH == 0:
                    wait(act, s_den, i * PAIRS_IN_BODY + p - 1)
                act.activation(a, a, ACT.Exp, bias=minrow[:, t % (MR // 2):t % (MR // 2) + 1], scale=-1.0,
                               accum_out=denhalf[:, p % 2, half, c, h:h + 1]).then_inc(s_exp, 1)

            def copy_b(i, m):
                u, c, half = m // UCH, (m % UCH) // 2, m % 2
                wait(act, s_trB, i * BCH + m + 1)
                if m % UCH == 0:
                    wait(act, s_pv, i * BU + u - 1)
                act.activation(
                    probT[:, u % 2, half * 8 + 4:half * 8 + 8, c * P:(c + 1) * P],
                    trB[:].rearrange("p (s t) -> p s t", t=P), ACT.Copy).then_inc(s_evB, 1)

            def copy_context(i, u):
                wait(act, s_pv, i * BU + u + 1)
                if u % HG == 0:
                    wait(act, s_sum, i * (BU // HG) + u // HG)
                act.activation(cpart[:, u % CR, :], pv[:, 0:PAIR], ACT.Copy).then_inc(s_ctx, 1)

            def slice_(i, n, first, over):
                def lagging(lag):
                    return not (first and n < lag) and not (over and n >= lag)

                if n % UCH == 0 and lagging(CTX_LAG):
                    copy_context(i, (n - CTX_LAG) // UCH)
                if lagging(EXP_LAG):
                    exps(i, n - EXP_LAG)
                if lagging(T_LAG):
                    copy_b(i, n - T_LAG)

            for n in range(BCH):
                slice_(0, n, True, False)
            with act.Fori(1, TRIPS) as i:
                for n in range(BCH):
                    slice_(i, n, False, False)
            for n in range(CTX_LAG + 1):
                slice_(TRIPS, n, False, True)

            def front(g):
                act.wait_ge(s_rt, g + 1)
                if g >= 1:
                    act.wait_ge(s_rb, g * DC)
                act.activation(rdT[:], bank[0][0:H, :], ACT.Copy).then_inc(s_rtc, 1)

            def mask3(g):
                for j in range(GB):
                    act.wait_ge(s_n2, GB * g + j + 1)
                    if g >= 2:
                        act.wait_ge(s_y2, GB * (g - 1))
                    act.activation(ht2[:, g % 2 * GB + j, :], hid[:, j, :], ACT.Copy,
                                   scale=nmaskf[:, g * GB + j:g * GB + j + 1]).then_inc(s_n3, 1)

            def copy3(g):
                for c in range(DC):
                    act.wait_ge(s_t3, DC * g + c + 1)
                    if g >= 1:
                        act.wait_ge(s_f1, FC * g)
                    act.activation(hidT[:, c, :], bank[2 + c], ACT.Copy).then_inc(s_c3, 1)

            def gelu(g):
                for f in range(FC):
                    act.wait_ge(s_f1, FC * g + f + 1)
                    if g >= 2:
                        act.wait_ge(s_f2, GB * (g - 1))
                    act.activation(gel[:, g % 2, f, :], bank[4 + f % 2], ACT.Gelu_apprx_tanh).then_inc(s_g, 1)

            act.wait_ge(s_sum, NPAIR * DC)
            front(0)
            mask3(0)
            copy3(0)
            for g in range(NG):
                if g + 1 < NG:
                    front(g + 1)
                gelu(g)
                if g + 1 < NG:
                    mask3(g + 1)
                    copy3(g + 1)

        @block.vector
        def _(dve):
            count = [0]

            def moments(k, src_stats, dst, s_dst):
                b = k % 2
                for j in range(GB):
                    dve.bn_stats(src_stats[:, j, :], tokens(k)[:, j, :]).then_inc(s_stat, 1)
                count[0] += GB
                dve.wait_ge(s_stat, count[0])
                for j in range(GB):
                    dve.bn_aggr(dst[:, b, j, :], src_stats[:, j, :]).then_inc(s_dst, 1)

            def moments_x(k):
                n = sources_until(k)
                dve.wait_ge(s_xin[k], 16)
                if n > 1:
                    dve.wait_ge(s_mv1, GB * (n - 1))
                if n > 2:
                    dve.wait_ge(s_r1, n - 2)
                moments(k, stats, mv, s_mv1)

            def moments_h(k):
                if is_source(k):
                    dve.wait_ge(s_relu, GB * sources_until(k))
                else:
                    dve.wait_ge(s_xin[k], 16)
                if k >= 1:
                    dve.wait_ge(s_mv2, GB * k)
                if k >= 2:
                    dve.wait_ge(s_r2, k - 1)
                moments(k, stats2, mv2, s_mv2)

            def shift(k):
                g = STEPS[k][1]
                for j in range(GB):
                    dve.wait_ge(s_sc, GB * k + j + 1)
                    t = tokens(k)[:, j, :]
                    dve.scalar_tensor_tensor(t, b1_bc, nmaskf[:, g * GB + j:g * GB + j + 1], t,
                                             ALU.mult, ALU.add).then_inc(s_ln, 1)

            def copy_turned(k):
                dve.wait_ge(s_tp, DC * k + 1)
                if k >= 2:
                    dve.wait_ge(s_prj, DC * (k - 1))
                    wait(dve, s_vp, GB * sources_until(k - 2))
                dve.tensor_copy(turned(k)[:, 0, :], bank[0]).then_inc(s_tcD, 1)

            def low(k):
                for c in range(DC):
                    s = k * DC + c
                    dve.wait_ge(s_hi, s + 1)
                    dve.tensor_tensor(ring_hl[:, s % FR, 1, :], ring_f[:, s % FR, :],
                                      ring_hl[:, s % FR, 0, :].bitcast(F32), ALU.subtract).then_inc(s_lo, 1)

            def copy_values(k):
                g, n = STEPS[k][1], sources_until(k) - 1
                for j in range(GB):
                    dve.wait_ge(s_vp, GB * n + j + 1)
                    if n == 0 and j == 0:
                        dve.wait_ge(s_w, 64)
                    dve.tensor_tensor(vals[:, g * GB + j, :], bank[4 + j][:, 0:D], bv_bc,
                                      ALU.add).then_inc(s_ve, 1)

            dve.wait_ge(s_rowsT, 1)
            dve.wait_ge(s_biases, 2)
            dve.tensor_copy(nmaskf[:], bank[7][:, 0:NB]).then_inc(s_rowsT, 1)
            dve.tensor_reduce(part_sel[:], ident[:].rearrange("p (j d) -> p d j", d=HD), AX.X,
                              ALU.add).then_inc(s_psel, 1)
            dve.wait_ge(s_w1, 32)
            for st in range(len(STEPS) + 5):
                if 0 <= st - 5:
                    low(st - 5)
                if 0 <= st - 4 < len(STEPS) and is_source(st - 4):
                    copy_values(st - 4)
                if 0 <= st - 3 < len(STEPS):
                    copy_turned(st - 3)
                if 0 <= st - 2 < len(STEPS):
                    shift(st - 2)
                if 0 <= st - 1 < len(STEPS):
                    moments_h(st - 1)
                if st < len(STEPS) and is_source(st):
                    moments_x(st)
            dve.wait_ge(s_adj0, 16)
            m0 = mask[:, 0, :, :].rearrange("p a n -> p (a n)")
            dve.tensor_scalar(m0, m0.bitcast(I32), 0.0, NEG, ALU.is_equal, ALU.mult).then_inc(s_m0, 1)
            dve.wait_ge(s_hts, 16 * NG)
            dve.wait_ge(s_tp, DC * len(STEPS))

            def copy_a(i, m):
                u, c, half = m // UCH, (m % UCH) // 2, m % 2
                if m % UCH == 0:
                    wait(dve, s_pv, i * BU + u - 1)
                wait(dve, s_trA, i * BCH + m + 1)
                dve.tensor_copy(
                    probT[:, u % 2, half * 8:half * 8 + 4, c * P:(c + 1) * P],
                    trA[:].rearrange("p (s t) -> p s t", t=P)).then_inc(s_evA, 1)

            def masked_min(i, n):
                t, half = n // 2, n % 2
                p, c = n // PCH, (n % UCH) // 2
                dve.tensor_tensor_reduce(
                    out=prob[:, t % PR, half * CH:(half + 1) * CH], in0=score[n % 2][:],
                    in1=mask[:, p % 2, c, half * CH:(half + 1) * CH], scale=1.0, scalar=HUGE,
                    op0=ALU.add, op1=ALU.min, accum_out=minhalf[:, n % MR:n % MR + 1]).then_inc(s_mx, 1)

            def copy_sum(i, v):
                wait(dve, s_sum, i * (BU // HG) + v + 1)
                wait(dve, s_cst[v % 2], 16 * (i * (BU // HG // 2) + v // 2))
                dve.tensor_copy(csum[:, v % 2, :], psum_sum[:, 0:PAIR]).then_inc(s_sumc, 1)

            def denominators(i, p):
                pair = i * PAIRS_IN_BODY + p
                wait(dve, s_exp, pair * PCH + PCH)
                d = denhalf[:, p % 2, :, :, :].rearrange("p a b h -> p a (b h)")
                o = den[:].rearrange("p b h -> p (b h)")[:, bass.ds(pair * 2 * H, 2 * H)]
                dve.tensor_tensor(o, d[:, 0, :], d[:, 1, :], ALU.add).then_inc(s_den, 1)

            def slice_(i, n, first, over):
                def lagging(lag):
                    return not (first and n < lag) and not (over and n >= lag)

                if lagging(T_LAG):
                    copy_a(i, n - T_LAG)
                if (n - SUM_COPY_LAG) % SCH == 0 and lagging(SUM_COPY_LAG):
                    copy_sum(i, (n - SUM_COPY_LAG) // SCH)
                if n % PCH == DEN_AT and not (first and n < PCH) and not (over and n >= PCH):
                    denominators(i, n // PCH - 1)
                if over:
                    return
                if first:
                    if n == 0:
                        dve.wait_ge(s_m0, 1)
                    if n == PCH:
                        dve.wait_ge(s_m, 16)
                    dve.wait_ge(s_qk, n + 1)
                elif n % PCH == 0:
                    dve.wait_ge(s_m, 16 * (i * PAIRS_IN_BODY + n // PCH))
                    dve.nop(nofuse=True)
                masked_min(i, n)

            for n in range(BCH):
                slice_(0, n, True, False)
            with dve.Fori(1, TRIPS) as i:
                for n in range(BCH):
                    slice_(i, n, False, False)
            for n in range(SUM_COPY_LAG):
                slice_(TRIPS, n, False, True)

            dve.wait_ge(s_den, NPAIR)
            dve.reciprocal(rden[:], den[:]).then_inc(s_rd, 1)

            def front(g):
                dve.wait_ge(s_cin[g], 16)
                cin = cin0 if g == 0 else cin_rest[:, g - 1, :, :]
                for c in range(DC):
                    dve.wait_ge(s_rb, DC * g + c + 1)
                    if g >= 1:
                        dve.wait_ge(s_wo, GB * g)
                    dve.tensor_tensor(cnorm[:, c, :], bank[2 + c], cin[:, c, :], ALU.mult).then_inc(s_cn, 1)

            def middle(g):
                for j in range(GB):
                    dve.wait_ge(s_wo, GB * g + 2 * (j // 2) + 2)
                    if g == 0 and j == 0:
                        dve.wait_ge(s_w3, 16 * 5)
                    if g >= 1:
                        dve.wait_ge(s_n3, GB * g)
                    dve.tensor_tensor(hid[:, j, :], bank[j // 2][:, D * (j % 2):D * (j % 2) + D], bo_bc,
                                      ALU.add).then_inc(s_h1, 1)
                for j in range(GB):
                    dve.wait_ge(s_h1, GB * g + j + 1)
                    tb = g * GB + j
                    dve.wait_ge(s_htin, 16 * (g + 1))
                    dve.scalar_tensor_tensor(hid[:, j, :], hid[:, j, :], nmaskf[:, tb:tb + 1], htin[:, j, :],
                                             ALU.mult, ALU.add).then_inc(s_h2, 1)
                back(g - 1, 0)
                b = g % 2
                for j in range(GB):
                    dve.wait_ge(s_h2, GB * g + j + 1)
                    if g >= 1:
                        dve.wait_ge(s_mv3, GB * g)
                    dve.bn_stats(stats[:, j, :], hid[:, j, :]).then_inc(s_st3, 1)
                for j in range(GB):
                    dve.wait_ge(s_st3, GB * g + j + 1)
                    dve.bn_aggr(mv[:, b, j, :], stats[:, j, :]).then_inc(s_mv3, 1)
                back(g - 1, 1)
                dve.wait_ge(s_mv3, GB * (g + 1))
                for j in range(GB):
                    dve.scalar_tensor_tensor(hid[:, j, :], hid[:, j, :], mv[:, b, j, 0:1], s2_bc,
                                             ALU.subtract, ALU.mult).then_inc(s_n1, 1)
                back(g - 1, 2)
                dve.wait_ge(s_r3, g + 1)
                for j in range(GB):
                    dve.wait_ge(s_n1, GB * g + j + 1)
                    dve.scalar_tensor_tensor(hid[:, j, :], hid[:, j, :], rstd[:, b, j:j + 1], b2_bc,
                                             ALU.mult, ALU.add).then_inc(s_n2, 1)

                back(g - 1, 3)

            def back(g, j):
                if g >= 0:
                    dve.wait_ge(s_f2, GB * g + j + 1)
                    r = ht2[:, g % 2 * GB + j, :]
                    dve.tensor_tensor(r, bank[6 + j % 2][:, 0:D], r, ALU.add).then_inc(s_y1, 1)

            for g in range(NG):
                front(g)
                middle(g)
            for j in range(GB):
                back(NG - 1, j)

        @block.tensor
        def _(pe):
            pe.wait_ge(s_ident, 1)
            pe.wait_ge(s_rows, 16 * 3)
            pe.wait_ge(s_rowsf, 1)
            pe.transpose(bank[7][:, 0:NB], nmask_r[:], ident[0:NB, 0:NB])
            pe.transpose(bank[7][:, NB:NB + 2 * DC], bias_r[:], ident[0:2 * DC, 0:2 * DC]).then_inc(s_rowsT, 1)

            def turn(k):
                for c in range(DC):
                    for j in range(GB):
                        if c == 0:
                            pe.wait_ge(s_ln, GB * k + j + 1)
                        if j == 0 and k >= 1:
                            pe.wait_ge((s_tcD, s_tcA)[c], k)
                        mm = pe.transpose(bank[c][:, j * P:(j + 1) * P], tokens(k)[:, j, c * P:(c + 1) * P],
                                          ident[:])
                    mm.then_inc(s_tp, 1)

            def project(k):
                w = wqkv[:, 1 if is_source(k) else 0, :, :]
                pe.wait_ge(s_tcD, k + 1)
                pe.wait_ge(s_tcA, k + 1)
                if k == 0:
                    pe.wait_ge(s_w, 64)
                for m in range(DC):
                    s = k * DC + m
                    if s >= 2:
                        pe.wait_ge(s_f, s - 1)
                    for c in range(DC):
                        mm = pe.matmul(bank[2 + s % 2], w[:, c, m * P:(m + 1) * P], turned(k)[:, c, :],
                                       start=(c == 0), stop=(c == DC - 1))
                    mm.then_inc(s_prj, 1)

            def project_values(k):
                n = sources_until(k) - 1
                if n == 0:
                    pe.wait_ge(s_rowsT, 2)
                    pe.wait_ge(s_biases, 2)
                for j in range(GB):
                    if n >= 1:
                        pe.wait_ge(s_ve, GB * (n - 1) + j + 1)
                    for c in range(DC):
                        mm = pe.matmul(bank[4 + j][:, 0:D], turned(k)[:, c, j * P:(j + 1) * P],
                                       wqkv[:, 2, c, :], start=(c == 0), stop=(c == DC - 1))
                    mm.then_inc(s_vp, 1)

            for k in range(len(STEPS)):
                turn(k)
                project(k)
                if is_source(k):
                    project_values(k)

            def scores(i, n):
                p, h, c, half = n // PCH, n // UCH % H, (n % UCH) // 2, n % 2
                wait(pe, s_mx, i * BCH + n - 1)
                for k in range(CH // GT):
                    at = half * CH + k * GT
                    mm = pe.matmul(score[n % 2][:, k * GT:(k + 1) * GT],
                                   qst[:, p % 2, h, c * P:(c + 1) * P], kst[:, h, at:at + GT],
                                   start=True, stop=True)
                mm.then_inc(s_qk, 1)

            def turn_probs(i, m):
                t, half = m // 2, m % 2
                wait(pe, s_exp, i * BCH + m + 1)
                for dst, s_free, s_done, b0 in ((trA, s_evA, s_trA, 0), (trB, s_evB, s_trB, 4)):
                    wait(pe, s_free, i * BCH + m)
                    for b in range(4):
                        at = (half * 8 + b0 + b) * P
                        mm = pe.transpose(dst[:, b * P:(b + 1) * P], prob[:, t % PR, at:at + P], ident[:])
                    mm.then_inc(s_done, 1)

            def context(i, u, k):
                h = u % H
                if k == 0:
                    wait(pe, s_evA, i * BCH + UCH * u + UCH)
                    wait(pe, s_evB, i * BCH + UCH * u + UCH)
                    wait(pe, s_ctx, i * BU + u)
                for j in range(HG):
                    sblk = HG * k + j
                    mm = pe.matmul(pv[HD * j:HD * (j + 1), 0:PAIR], vals[:, sblk, h * HD:(h + 1) * HD],
                                   probT[:, u % 2, sblk, :], start=(k == 0), stop=(k == NB // HG - 1))
                if k == NB // HG - 1:
                    mm.then_inc(s_pv, 1)

            def sum_parts(i, v):
                wait(pe, s_ctx, i * BU + HG * (v + 1))
                wait(pe, s_sumc, i * (BU // HG) + v)
                for j in range(HG):
                    mm = pe.matmul(psum_sum[HD * j:HD * (j + 1), 0:PAIR], part_sel[:], cpart[:, j, :],
                                   start=True, stop=True)
                mm.then_inc(s_sum, 1)

            def slice_(i, n, first, over):
                def lagging(lag):
                    return not (first and n < lag) and not (over and n >= lag)

                if not over:
                    if n % PCH == 0:
                        pe.wait_ge(s_qst[n // PCH], 64 * (i + 1))
                    if first and n % UCH == 0:
                        for k, (h0, _) in enumerate(KHEADS):
                            if n == UCH * h0:
                                pe.wait_ge(s_kst[k], 64)
                    scores(i, n)
                if lagging(T_LAG):
                    turn_probs(i, n - T_LAG)
                if lagging(PV_LAG):
                    context(i, (n - PV_LAG) // UCH, (n - PV_LAG) % UCH)
                if (n - SUM_LAG) % SCH == 0 and lagging(SUM_LAG):
                    sum_parts(i, (n - SUM_LAG) // SCH)

            pe.wait_ge(s_f, len(STEPS) * DC)
            pe.wait_ge(s_ve, GB * NG)
            pe.wait_ge(s_psel, 1)
            for n in range(BCH):
                slice_(0, n, True, False)
            with pe.Fori(1, TRIPS) as i:
                for n in range(BCH):
                    slice_(i, n, False, False)
            for n in range(SUM_LAG):
                slice_(TRIPS, n, False, True)

            pe.wait_ge(s_mx, NPAIR * PCH)
            pe.wait_ge(s_evA, NPAIR * PCH)
            pe.wait_ge(s_evB, NPAIR * PCH)
            pe.wait_ge(s_ctx, NPAIR * H)
            pe.wait_ge(s_sumc, NPAIR * DC)
            pe.wait_ge(s_const, 2)

            def front(g):
                pe.wait_ge(s_rd, 1)
                if g >= 1:
                    pe.wait_ge(s_h1, GB * g)
                for j in range(GB):
                    mm = pe.transpose(bank[0][0:H, j * P:(j + 1) * P], rden[:, g * GB + j, :], ident[:])
                mm.then_inc(s_rt, 1)
                pe.wait_ge(s_rtc, g + 1)
                if g >= 1:
                    pe.wait_ge(s_c3, DC * g)
                for c in range(DC):
                    pe.matmul(bank[2 + c], head_sel[:, c * P:(c + 1) * P], rdT[:],
                              start=True, stop=True).then_inc(s_rb, 1)

            def project_out(g):
                pe.wait_ge(s_wol, 16)
                pe.wait_ge(s_cn, DC * (g + 1))
                for j in range(GB):
                    for c in range(DC):
                        mm = pe.matmul(bank[j // 2][:, D * (j % 2):D * (j % 2) + D],
                                       cnorm[:, c, j * P:(j + 1) * P], wo[:, c, :],
                                       start=(c == 0), stop=(c == DC - 1))
                    mm.then_inc(s_wo, 1)

            def turn3(g):
                for c in range(DC):
                    for j in range(GB):
                        if c == 0:
                            pe.wait_ge(s_n3, GB * g + j + 1)
                        if g >= 1 and j == 0:
                            pe.wait_ge(s_c3, DC * (g - 1) + c + 1)
                        mm = pe.transpose(bank[2 + c][:, j * P:(j + 1) * P],
                                          ht2[:, g % 2 * GB + j, c * P:(c + 1) * P], ident[:])
                    mm.then_inc(s_t3, 1)

            def ffn1(g):
                pe.wait_ge(s_c3, DC * (g + 1))
                if g == 0:
                    pe.wait_ge(s_w3, 16 * 5)
                for f in range(FC):
                    if g * FC + f >= 2:
                        pe.wait_ge(s_g, g * FC + f - 1)
                    for c in range(DC):
                        mm = pe.matmul(bank[4 + f % 2], w1[:, c, f * P:(f + 1) * P], hidT[:, c, :],
                                       start=(c == 0), stop=(c == DC - 1))
                    mm.then_inc(s_f1, 1)

            def ffn2(g):
                pe.wait_ge(s_g, FC * (g + 1))
                for j in range(GB):
                    if GB * g + j >= 2:
                        pe.wait_ge(s_y1, GB * g + j - 1)
                    for f in range(FC):
                        mm = pe.matmul(bank[6 + j % 2][:, 0:D], gel[:, g % 2, f, j * P:(j + 1) * P],
                                       w2[:, f, :], start=(f == 0), stop=(f == FC - 1))
                    mm.then_inc(s_f2, 1)

            front(0)
            project_out(0)
            turn3(0)
            for g in range(NG):
                if g + 1 < NG:
                    front(g + 1)
                ffn1(g)
                if g + 1 < NG:
                    project_out(g + 1)
                ffn2(g)
                if g + 1 < NG:
                    turn3(g + 1)


_INS = ["x", "adj", "nodemask", "L0_gnn_h_target", "L0_gnn_ln1_scale", "L0_gnn_ln1_bias",
        "L0_gnn_Wq", "L0_gnn_bq", "L0_gnn_Wk", "L0_gnn_bk", "L0_gnn_Wv", "L0_gnn_bv", "L0_gnn_Wo",
        "L0_gnn_bo", "L0_gnn_ln2_scale", "L0_gnn_ln2_bias", "L0_gnn_W1", "L0_gnn_W2"]


def kernel(**inputs):
    import numpy as np
    import concourse.bacc as bacc
    from concourse.bass_utils import run_bass_kernel_spmd

    nc = bacc.Bacc("TRN2", target_bir_lowering=False, num_devices=1)
    arrays, args = {}, []
    for name in _INS:
        a = np.ascontiguousarray(inputs[name])
        arrays[f"in_{name}"] = a
        args.append(nc.dram_tensor(f"in_{name}", a.shape, mybir.dt.from_np(a.dtype), kind="ExternalInput").ap())
    out = nc.dram_tensor("out_0", (N, D), F32, kind="ExternalOutput").ap()
    program(nc, *args, out)
    r = run_bass_kernel_spmd(nc, [arrays], core_ids=[0])
    return r.results[0]["out_0"]
```

```python
from contextlib import ExitStack

import concourse.bass as bass
from concourse import mybir

ALU = mybir.AluOpType
ACT = mybir.ActivationFunctionType
AX = mybir.AxisListType
F32 = mybir.dt.float32
F32R = mybir.dt.float32r
I32 = mybir.dt.int32

P = 128
N = 2048
D = 256
H = 8
HD = D // H
F = 4 * D
EPS = 1e-5
NEG = 1e30
HUGE = 3e38
QSCALE = -float(HD) ** -0.5

NB = N // P
DC = D // P
FC = F // P
GT = 512
GB = GT // P
NG = N // GT
HG = P // HD

PAIR = 2 * P
NPAIR = N // PAIR
CH = 1024
UCH = 2 * N // CH
PCH = UCH * H
PAIRS_IN_BODY = 2
BCH = PAIRS_IN_BODY * PCH
BU = PAIRS_IN_BODY * H
TRIPS = NPAIR // PAIRS_IN_BODY

EXP_LAG = 3
T_LAG = 4
PV_LAG = T_LAG + UCH
CTX_LAG = PV_LAG + UCH
SUM_LAG = CTX_LAG + UCH * (HG - 1) + 1
SUM_COPY_LAG = SUM_LAG + 1
DEN_AT = EXP_LAG + 4
SCH = UCH * HG
TURN_AT, COPY_AT, SPREAD_AT, NORM_AT, OUT_AT, MIDDLE_AT = 1, 2, 3, 4, 5, 9

PR = 4
MR = 16
CR = HG
FR = 4

POOL_LOW = (1, 3)
VECTOR_LOW = tuple(f for f in range(FC) if f not in POOL_LOW)


def program(nc, x, adj, nodemask, h_target, ln1_scale, ln1_bias, Wq, bq, Wk, bk, Wv, bv, Wo, bo,
            ln2_scale, ln2_bias, W1, W2, out):
    with ExitStack() as ctx:
        def sb(name, shape, dt=F32):
            return ctx.enter_context(nc.sbuf_tensor(name, shape, dt))

        def sem(name):
            return ctx.enter_context(nc.semaphore(name))

        parts_scr = nc.dram_tensor("parts_scr", (2, 2, D, N), F32).ap()
        ctx_scr = nc.dram_tensor("ctx_scr", (D, N), F32).ap()
        ht_scr = nc.dram_tensor("ht_scr", (N, D), F32).ap()

        kst = sb("kst", [P, H, N], F32R)
        qst = sb("qst", [P, 2, H, PAIR], F32R)
        vals = sb("vals", [P, NB, D])
        prob = sb("prob", [P, PR, N])
        probT = sb("probT", [P, 2, NB, PAIR])
        mask = sb("mask", [P, 2, 2, N])
        cpart = sb("cpart", [P, CR, PAIR])
        csum = sb("csum", [P, 2, PAIR])
        cin0 = sb("cin0", [P, DC, GT])
        ident = sb("ident", [P, P])
        part_sel = sb("part_sel", [P, HD])
        head_sel_r = sb("head_sel_r", [H, D], F32R)
        minhalf = sb("minhalf", [P, MR])
        minrow = sb("minrow", [P, MR // 2])
        denhalf = sb("denhalf", [P, 2, 2, 2, H])
        den = sb("den", [P, NB, H])
        rden = sb("rden", [P, NB, H])
        half_neg = sb("half_neg", [P, GB])
        nmask_i = sb("nmask_i", [NB, P], I32)
        nmask_r = sb("nmask_r", [NB, P])
        bias_r = sb("bias_r", [2 * DC, P])
        nmaskf = sb("nmaskf", [P, NB])
        kbias = sb("kbias", [P, DC])
        qbias_s = sb("qbias_s", [P, DC])
        stats = sb("stats", [P, GB, 6])
        stats2 = sb("stats2", [P, GB, 6])
        mv = sb("mv", [P, 2, GB, 2])
        mv2 = sb("mv2", [P, 2, GB, 2])
        vareps = sb("vareps", [P, 2, GB])
        rstd = sb("rstd", [P, 2, GB])
        rstd1 = sb("rstd1", [P, 2, GB])
        nbias = sb("nbias", [P, 2, GB])
        nbias1 = sb("nbias1", [P, 2, GB])
        tmpa = sb("tmpa", [P, GB])
        tmpb = sb("tmpb", [P, GB])
        tmpc = sb("tmpc", [P, GB])

        xs = prob[:, 0:2, :].rearrange("p a (b d) -> p (a b) d", d=D)
        turned_ring = prob[:, 2, :].rearrange("p (r c n) -> p r c n", r=2, c=DC)
        spare = probT[:, 1, :, :].rearrange("p b t -> p (b t)")
        ring_f = spare[:, 0:FR * GT].rearrange("p (r n) -> p r n", r=FR)
        ofs = FR * GT
        s1_bc = spare[:, ofs:ofs + D]
        b1_bc = spare[:, ofs + D:ofs + 2 * D]
        ofs += 2 * D
        wqkv = spare[:, ofs:ofs + 3 * DC * D].rearrange("p (w c n) -> p w c n", w=3, c=DC)
        cspare = cpart[:, :, :].rearrange("p r t -> p (r t)")
        bv_bc = cspare[:, 0:D]
        head_sel = cspare[0:H, D:2 * D]
        ring_hl = mask[:, 1, :, :].rearrange("p a n -> p (a n)").bitcast(F32R).rearrange(
            "p (r s n) -> p r s n", r=FR, s=2)

        w12 = mask[:, 0, :, :]
        w12h = qst[:, :, :, :].rearrange("p b h t -> p b (h t)")
        k1 = kst[:, :, :].rearrange("p h n -> p (h n)")
        gelh, gell = (k1[:, s * FC * GT:(s + 1) * FC * GT].rearrange("p (c n) -> p c n", c=FC)
                      for s in range(2))
        ofs = 2 * FC * GT
        w12l = k1[:, ofs:ofs + 2 * FC * D].rearrange("p (w n) -> p w n", w=2)
        ofs += 2 * FC * D
        hidTh, hidTl = (k1[:, ofs + s * DC * GT:ofs + (s + 1) * DC * GT].rearrange("p (c n) -> p c n", c=DC)
                        for s in range(2))
        w1h, w1l = (w[:, 0, :].rearrange("p (c f) -> p c f", c=DC) for w in (w12h, w12l))
        w2h, w2l = (w[:, 1, :].rearrange("p (c d) -> p c d", c=FC) for w in (w12h, w12l))
        ofs += 2 * DC * GT
        rdT = k1[0:H, ofs:ofs + 4 * GT].rearrange("p (g s n) -> p g s n", g=2, s=2)
        gel = prob[:, 0:2, :].rearrange("p a (c n) -> p (a c) n", n=GT)
        htin = prob[:, 2, 0:GB * D].rearrange("p (b d) -> p b d", d=D)
        cin_rest = probT[:, :, :, :].rearrange("p b s t -> p (b s t)")[:, 0:(NG - 1) * DC * GT].rearrange(
            "p (g c n) -> p g c n", g=NG - 1, c=DC)
        cins = [cin0[:]] + [cin_rest[:, g, :, :] for g in range(NG - 1)]
        m1 = mask[:, 1, :, :].rearrange("p a n -> p (a n)")
        s2_bc = m1[:, 0:D]
        b2_bc = m1[:, D:2 * D]
        bo_bc = m1[:, 2 * D:3 * D]
        hid = m1[:, 1024:2048].rearrange("p (b d) -> p b d", d=D)
        xres = m1[:, 3072:4096].rearrange("p (b d) -> p b d", d=D)
        ht2 = vals[:, 0:2 * GB, :]
        wo = m1[:, 2048:2048 + DC * D].rearrange("p (c n) -> p c n", c=DC)

        score = [ctx.enter_context(nc.psum_tensor(f"score{i}", [P, CH], F32)) for i in range(2)]
        trA = ctx.enter_context(nc.psum_tensor("trA", [P, GT], F32))
        trB = ctx.enter_context(nc.psum_tensor("trB", [P, GT], F32))
        pv = ctx.enter_context(nc.psum_tensor("pv", [P, GT], F32))
        psum_sum = ctx.enter_context(nc.psum_tensor("psum_sum", [P, GT], F32))
        bank = [score[0][:, 0:GT], score[0][:, GT:CH], score[1][:, 0:GT], score[1][:, GT:CH],
                trA[:, :], trB[:, :], pv[:, :], psum_sum[:, :]]

        s_rows = sem("mask_and_biases_loaded")
        s_w1 = sem("ln1_loaded")
        s_w = sem("weights_loaded")
        s_ident = sem("identity_ready")
        s_rowsf = sem("mask_as_float")
        s_rowsT = sem("mask_and_biases_turned")
        s_xin = [sem(f"group_loaded{g}") for g in range(2 * NG)]
        s_adj0 = sem("adj_loaded0")
        s_adj1 = sem("adj_loaded1")
        s_psel = sem("part_selector_ready")
        s_biases = sem("biases_copied")
        s_zero = sem("constants_zeroed")
        s_const = sem("constants_ready")
        s_stat = sem("stats_taken")
        s_mv1 = sem("moments_x")
        s_mv2 = sem("moments")
        s_pc = sem("pool_small_step")
        s_r1 = sem("rstd_x_ready")
        s_r2 = sem("rstd_ready")
        s_relu = sem("relu_done")
        s_xn = sem("normalised")
        s_sc = sem("scaled")
        s_ln = sem("ln1_done")
        s_tp = sem("rows_transposed")
        s_tcD = sem("transposes_copied_vector")
        s_tcA = sem("transposes_copied_scalar")
        s_prj = sem("projected")
        s_vp = sem("values_projected")
        s_f = sem("projection_copied")
        s_hi = sem("high_part")
        s_lo = sem("low_part")
        s_ve = sem("values_copied")
        s_parts = [sem(f"parts_stored{r}") for r in range(FR)]
        s_kst = sem("keys_stacked")
        s_qst = [sem(f"queries_stacked{b}") for b in range(2)]
        s_hts = sem("targets_stored")
        s_htin = sem("targets_loaded")
        s_m0 = sem("first_mask_ready")
        s_m = sem("mask_ready")
        s_qk = sem("scores_ready")
        s_mx = sem("minimum_taken")
        s_nm = sem("minimum_of_row")
        s_exp = sem("exp_done")
        s_trA = sem("transposed_a")
        s_trB = sem("transposed_b")
        s_evA = sem("copied_a")
        s_evB = sem("copied_b")
        s_pv = sem("context_summed")
        s_ctx = sem("context_copied")
        s_sum = sem("parts_summed")
        s_sumc = sem("sums_copied")
        s_cst = [sem(f"context_stored{r}") for r in range(2)]
        s_den = sem("denominators")
        s_wol = sem("output_weights_loaded")
        s_w3 = sem("ln2_and_bias_loaded")
        s_w1l = sem("ffn_weights1_loaded")
        s_w2l = sem("ffn_weights2_loaded")
        s_w1s = sem("ffn_weights1_split")
        s_w2s = sem("ffn_weights2_split")
        s_cin = [sem(f"context_loaded{g}") for g in range(NG)]
        s_xr = sem("x_loaded")
        s_rd = sem("reciprocals")
        s_rt = sem("reciprocals_transposed")
        s_rtc = sem("reciprocals_high_part")
        s_rtl = sem("reciprocals_low_part")
        s_hsel = sem("head_selector_ready")
        s_rb = sem("reciprocals_spread")
        s_cn = sem("context_normalised")
        s_wo = sem("output_projected")
        s_h1 = sem("bias_added")
        s_h2 = sem("residual_added")
        s_st3 = sem("stats_taken3")
        s_mv3 = sem("moments3")
        s_p3 = sem("pool_small_step3")
        s_r3 = sem("rstd3_ready")
        s_n1 = sem("centred3")
        s_n2 = sem("ln2_affine")
        s_n3 = sem("ln2_masked")
        s_t3 = sem("ln2_transposed")
        s_c3 = sem("ln2_high_part")
        s_c3l = sem("ln2_low_part")
        s_f1 = sem("ffn1_done")
        s_g = sem("gelu_done")
        s_gl = sem("gelu_low_part_vector")
        s_glp = sem("gelu_low_part_pool")
        s_f2 = sem("ffn2_done")
        s_y1 = sem("ffn_added")
        s_y2 = sem("x_added")
        s_out = sem("out_stored")

        def rows(a, g):
            return a.rearrange("(b p) d -> p b d", p=P)[:, g * GB:(g + 1) * GB, :]

        def wait(eng, s, value):
            if isinstance(value, int) and value <= 0:
                return
            eng.wait_ge(s, value)

        block = ctx.enter_context(nc.Block())

        STEPS = [("t", 0)] + [("s", g) for g in range(NG)] + [("t", g) for g in range(1, NG)]
        SLOTS = NG
        SOURCES = [k for k, (kind, _) in enumerate(STEPS) if kind == "s"]
        LAST_SOURCE = SOURCES[-1]

        def is_source(k):
            return STEPS[k][0] == "s"

        def sources_until(k):
            return sum(1 for j in SOURCES if j <= k)

        def targets_until(k):
            return k + 1 - sources_until(k)

        def tokens(k):
            return xs[:, k % SLOTS * GB:(k % SLOTS + 1) * GB, :]

        def turned(k):
            return turned_ring[:, k % 2, :, :]

        def slot_uses(r, s):
            return len([q for q in range(s) if q % FR == r])

        QUADRANTS = {1: (0, 1, 0, 1), 0: (0, 0, 1, 1)}

        def load_adj(sp, pair, s):
            b = 0 if s is s_adj0 else 1
            sp.dma_start(
                mask[:, b, :, :].bitcast(I32),
                adj[bass.ds(pair * PAIR, PAIR), :].rearrange("(b p) n -> p b n", p=P)).then_inc(s, 16)

        def load_queries(sp, pair, b):
            for quad in range(4):
                sp.dma_start(
                    qst[HD * quad:HD * (quad + 1), b, :, :].bitcast(F32),
                    parts_scr[0, QUADRANTS[0][quad], :, bass.ds(pair * PAIR, PAIR)].rearrange(
                        "(h d) n -> d h n", d=HD)).then_inc(s_qst[b], 16)

        @block.sync
        def _(sp):
            def load_rows(k):
                kind, g = STEPS[k]
                sp.dma_start(tokens(k), rows(x if kind == "s" else h_target, g)).then_inc(s_xin[k], 16)

            load_rows(0)
            load_rows(1)
            sp.dma_start(nmask_i[:], nodemask.rearrange("(b p) -> b p", p=P)).then_inc(s_rows, 16)
            sp.dma_start(bias_r[0:DC, :], bq.rearrange("(c p) -> c p", p=P)).then_inc(s_rows, 16)
            sp.dma_start(bias_r[DC:2 * DC, :], bk.rearrange("(c p) -> c p", p=P)).then_inc(s_rows, 16)
            sp.dma_start(s1_bc, ln1_scale.rearrange("(a d) -> a d", a=1).to_broadcast([P, D])).then_inc(s_w1, 16)
            sp.dma_start(b1_bc, ln1_bias.rearrange("(a d) -> a d", a=1).to_broadcast([P, D])).then_inc(s_w1, 16)
            load_rows(2)
            for j, w in enumerate((Wq, Wk, Wv)):
                sp.dma_start(wqkv[:, j, :, :], w.rearrange("(c p) n -> p c n", p=P)).then_inc(s_w, 16)
            sp.dma_start(bv_bc, bv.rearrange("(a d) -> a d", a=1).to_broadcast([P, D])).then_inc(s_w, 16)
            load_rows(3)
            load_adj(sp, 0, s_adj0)
            def stack_keys(k):
                for s in range(k * DC, (k + 1) * DC):
                    sp.wait_ge(s_parts[s % FR], 16 * slot_uses(s % FR, s + 1))
                at = STEPS[k][1] * GT
                for quad in range(4):
                    sp.dma_start(
                        kst[HD * quad:HD * (quad + 1), :, at:at + GT].bitcast(F32),
                        parts_scr[1, QUADRANTS[1][quad], :, at:at + GT].rearrange(
                            "(h d) n -> d h n", d=HD)).then_inc(s_kst, 16)

            for s in range(len(STEPS) * DC):
                k, c = s // DC, s % DC
                kind, g = STEPS[k]
                which = 1 if kind == "s" else 0
                if c == 0:
                    if kind == "t":
                        sp.wait_ge(s_ln, GB * (k + 1))
                        sp.dma_start(rows(ht_scr, g), tokens(k)).then_inc(s_hts, 16)
                    if k + SLOTS < len(STEPS):
                        sp.wait_ge(s_tp, DC * (k + 1))
                        if kind == "t":
                            sp.wait_ge(s_hts, 16 * targets_until(k))
                        load_rows(k + SLOTS)
                sp.wait_ge(s_lo, s + 1)
                sp.wait_ge(s_hi, s + 1)
                sp.dma_start(
                    parts_scr[which, :, c * P:(c + 1) * P, g * GT:(g + 1) * GT].rearrange("s p n -> p s n"),
                    ring_hl[:, s % FR, :, :].bitcast(F32)).then_inc(s_parts[s % FR], 16)
                if c == DC - 1 and k >= 1 and is_source(k - 1):
                    stack_keys(k - 1)
                if c == DC - 1 and k == LAST_SOURCE + 1:
                    load_queries(sp, 0, 0)
            for r in range(FR):
                sp.wait_ge(s_parts[r], 16 * slot_uses(r, len(STEPS) * DC))
            load_adj(sp, 1, s_adj1)
            load_queries(sp, 1, 1)

            def store(i, v):
                p, c = v // DC, v % DC
                pair = i * PAIRS_IN_BODY + p
                sp.wait_ge(s_sumc, i * (BU // HG) + v + 1)
                sp.nop(nofuse=True)
                sp.dma_start(ctx_scr[c * P:(c + 1) * P, bass.ds(pair * PAIR, PAIR)],
                             csum[:, v % 2, :]).then_inc(s_cst[v % 2], 16)

            def refill(i, p):
                pair = i * PAIRS_IN_BODY + p
                sp.wait_ge(s_mx, pair * PCH + PCH)
                sp.nop(nofuse=True)
                load_adj(sp, pair + 2, (s_adj0, s_adj1)[p])
                sp.wait_ge(s_qk, pair * PCH + PCH)
                sp.nop(nofuse=True)
                load_queries(sp, pair + 2, p)

            def body(i, first, last):
                for p in range(PAIRS_IN_BODY):
                    if not (first and p == 0):
                        store(i, DC * p - 1)
                    store(i, DC * p)
                    if not last:
                        refill(i, p)

            body(0, True, False)
            with sp.Fori(1, TRIPS - 1) as i:
                body(i, False, False)
            body(TRIPS - 1, False, True)

            def load_context(g):
                sp.dma_start(cins[g], ctx_scr[:, g * GT:(g + 1) * GT].rearrange("(c p) n -> p c n", p=P)
                             ).then_inc(s_cin[g], 16)

            for r in range(2):
                sp.wait_ge(s_cst[r], 16 * (NPAIR * DC // 2 - 1))
            load_context(0)
            sp.wait_ge(s_mx, (NPAIR - 1) * PCH)
            for j, (w, s) in enumerate(((W1, s_w1l), (W2, s_w2l))):
                sp.dma_start(w12[:, j, :].rearrange("p (c f) -> p c f", f=w.shape[1]),
                             w.rearrange("(c p) f -> p c f", p=P)).then_inc(s, 16)
            sp.wait_ge(s_mx, NPAIR * PCH)
            sp.dma_start(wo, Wo.rearrange("(c p) n -> p c n", p=P)).then_inc(s_wol, 16)
            for dst, v in ((s2_bc, ln2_scale), (b2_bc, ln2_bias), (bo_bc, bo)):
                sp.dma_start(dst, v.rearrange("(a d) -> a d", a=1).to_broadcast([P, D])).then_inc(s_w3, 16)
            sp.wait_ge(s_trB, NPAIR * PCH)
            sp.dma_start(htin, rows(ht_scr, 0)).then_inc(s_htin, 16)
            sp.wait_ge(s_pv, NPAIR * H)
            for g in range(1, NG - 1):
                load_context(g)
            store(TRIPS, -1)
            for r in range(2):
                sp.wait_ge(s_cst[r], 16 * (NPAIR * DC // 2))
            load_context(NG - 1)
            for g in range(NG):
                if g >= 1:
                    sp.wait_ge(s_out, 16 * g)
                sp.dma_start(xres, rows(x, g)).then_inc(s_xr, 16)
                if g + 1 < NG:
                    sp.wait_ge(s_h2, GB * (g + 1))
                    sp.dma_start(htin, rows(ht_scr, g + 1)).then_inc(s_htin, 16)
                if g + 1 < NG:
                    sp.wait_ge(s_y2, GB * (g + 1))
                    sp.dma_start(rows(out, g), xres).then_inc(s_out, 16)
            for j in range(GB):
                sp.wait_ge(s_y2, GB * (NG - 1) + j + 1)
                sp.dma_start(rows(out, NG - 1)[:, j, :], xres[:, j, :]).then_inc(s_out, 16)
            sp.wait_ge(s_out, 16 * (NG - 1 + GB))

        @block.gpsimd
        def _(pool):
            pool.memset(ident[:], 0.0).then_inc(s_zero, 1)
            pool.memset(head_sel, 0.0).then_inc(s_zero, 1)
            pool.memset(half_neg[:], -0.5).then_inc(s_const, 1)
            pool.wait_ge(s_zero, 1)
            pool.affine_select(out=ident[:], in_=ident[:], compare_op=ALU.not_equal, fill=1.0, base=0,
                               pattern=[[-1, P]], channel_multiplier=1).then_inc(s_ident, 1)
            pool.wait_ge(s_rows, 16 * 3)
            pool.tensor_scalar(nmask_r[:], nmask_i[:], 1.0, None, ALU.is_equal).then_inc(s_rowsf, 1)
            pool.wait_ge(s_zero, 2)
            pool.affine_select(out=head_sel.rearrange("h (g d) -> h g d", d=HD),
                               in_=head_sel.rearrange("h (g d) -> h g d", d=HD),
                               compare_op=ALU.not_equal, fill=1.0, base=0,
                               pattern=[[-1, H], [0, HD]], channel_multiplier=1).then_inc(s_const, 1)
            pool.wait_ge(s_const, 1)

            PIECES = 16
            step = [0]

            def small(ins):
                step[0] += 1
                ins.then_inc(s_pc, 1)
                pool.wait_ge(s_pc, step[0])

            def root(var, b, dst):
                small(pool.tensor_scalar(vareps[:, b, :], var, EPS, None, ALU.add))
                small(pool.tensor_tensor(dst, vareps[:, b, :], half_neg[:], ALU.pow))

            def norm_x(k):
                b, n = k % 2, sources_until(k)
                pool.wait_ge(s_mv1, GB * n)
                if n > 2:
                    pool.wait_ge(s_relu, GB * (n - 2))
                root(mv[:, b, :, 1], b, rstd1[:, b, :])
                small(pool.tensor_tensor(tmpa[:], mv[:, b, :, 0], rstd1[:, b, :], ALU.mult))
                pool.tensor_scalar(nbias1[:, b, :], tmpa[:], -1.0, None, ALU.mult).then_inc(s_r1, 1)

            def norm(k):
                b, g = k % 2, STEPS[k][1]
                pool.wait_ge(s_mv2, GB * (k + 1))
                if k >= 2:
                    pool.wait_ge(s_xn, GB * (k - 1))
                if k == 0:
                    pool.wait_ge(s_rowsT, 2)
                root(mv2[:, b, :, 1], b, tmpb[:])
                small(pool.tensor_tensor(rstd[:, b, :], tmpb[:], nmaskf[:, g * GB:(g + 1) * GB], ALU.mult))
                small(pool.tensor_tensor(tmpc[:], mv2[:, b, :, 0], rstd[:, b, :], ALU.mult))
                pool.tensor_scalar(nbias[:, b, :], tmpc[:], -1.0, None, ALU.mult).then_inc(s_r2, 1)

            def scale(k):
                if k == 0:
                    pool.wait_ge(s_w1, 32)
                for j in range(GB):
                    pool.wait_ge(s_xn, GB * k + j + 1)
                    t = tokens(k)[:, j, :]
                    pool.tensor_tensor(t, t, s1_bc, ALU.mult).then_inc(s_sc, 1)

            def convert(b, k, s, count):
                w = 2 * N // PIECES
                a = mask[:, b, :, :].rearrange("p a n -> p (a n)")[:, k * w:(k + 1) * w]
                pool.wait_ge(s, count)
                pool.nop(nofuse=True)
                pool.tensor_scalar(a, a.bitcast(I32), 0.0, NEG, ALU.is_equal, ALU.mult).then_inc(s_m, 1)

            for st in range(len(STEPS) + 1):
                if st < len(STEPS) and is_source(st):
                    norm_x(st)
                if 0 <= st - 1:
                    norm(st - 1)
                if 0 <= st - 1:
                    scale(st - 1)

            def body(i, last):
                for t in range(BCH // 2):
                    p, j = t // (PCH // 2), t % (PCH // 2)
                    pp = (p - 1) % 2
                    fresh = not (last and p == 1)
                    pool.wait_ge(s_mx, i * BCH + 2 * t + 2)
                    if t >= MR // 2 or not (isinstance(i, int) and i == 0):
                        pool.wait_ge(s_exp, i * BCH + 2 * t - MR + 2)
                    pool.nop(nofuse=True)
                    pool.tensor_scalar(minrow[:, t % (MR // 2):t % (MR // 2) + 1],
                                       minhalf[:, 2 * t % MR:2 * t % MR + 1],
                                       minhalf[:, (2 * t + 1) % MR:(2 * t + 1) % MR + 1], None,
                                       ALU.min).then_inc(s_nm, 1)
                    if fresh and 5 <= j < 5 + PIECES // 2:
                        load = 16 * (i + 2) if p == 1 else 16 * (i + 1)
                        for k in (2 * (j - 5), 2 * (j - 5) + 1):
                            convert(pp, k, (s_adj0, s_adj1)[pp], load)

            body(0, False)
            with pool.Fori(1, TRIPS - 1) as i:
                body(i, False)
            body(TRIPS - 1, True)

            def norm3(g):
                b = g % 2
                pool.wait_ge(s_mv3, GB * (g + 1))
                small3(pool.tensor_scalar(vareps[:, b, :], mv[:, b, :, 1], EPS, None, ALU.add))
                if g >= 2:
                    pool.wait_ge(s_n2, GB * (g - 1))
                pool.tensor_tensor(rstd[:, b, :], vareps[:, b, :], half_neg[:], ALU.pow).then_inc(s_r3, 1)

            step3 = [0]

            def small3(ins):
                step3[0] += 1
                ins.then_inc(s_p3, 1)
                pool.wait_ge(s_p3, step3[0])

            def add_x(g):
                for j in range(GB):
                    pool.wait_ge(s_y1, GB * g + j + 1)
                    pool.wait_ge(s_xr, 16 * (g + 1))
                    pool.tensor_tensor(xres[:, j, :], xres[:, j, :], ht2[:, g % 2 * GB + j, :], ALU.add).then_inc(s_y2, 1)

            def low_weights(j, s):
                pool.wait_ge(s, 1)
                pool.tensor_tensor(w12l[:, j, :], w12[:, j, :], w12h[:, j, :].bitcast(F32),
                                   ALU.subtract).then_inc(s, 1)

            def gelu_low(g):
                for f in POOL_LOW:
                    pool.wait_ge(s_g, 2 * (FC * g + f + 1))
                    pool.tensor_tensor(gell[:, f, :], gel[:, f, :], gelh[:, f, :].bitcast(F32),
                                       ALU.subtract).then_inc(s_glp, 1)

            low_weights(0, s_w1s)
            norm3(0)
            low_weights(1, s_w2s)
            for g in range(NG):
                gelu_low(g)
                if g + 1 < NG:
                    norm3(g + 1)
                add_x(g)

        @block.scalar
        def _(act):
            act.wait_ge(s_rowsT, 1)
            act.activation(qbias_s[:], bank[7][:, NB:NB + DC], ACT.Copy, scale=QSCALE).then_inc(s_biases, 1)
            act.activation(kbias[:], bank[7][:, NB + DC:NB + 2 * DC], ACT.Copy).then_inc(s_biases, 1)

            def relu(k):
                b, n = k % 2, sources_until(k)
                act.wait_ge(s_r1, n)
                for j in range(GB):
                    t = tokens(k)[:, j, :]
                    act.activation(t, t, ACT.Relu, bias=nbias1[:, b, j:j + 1],
                                   scale=rstd1[:, b, j:j + 1]).then_inc(s_relu, 1)

            def normalise(k):
                b = k % 2
                act.wait_ge(s_r2, k + 1)
                for j in range(GB):
                    t = tokens(k)[:, j, :]
                    act.activation(t, t, ACT.Identity, bias=nbias[:, b, j:j + 1],
                                   scale=rstd[:, b, j:j + 1]).then_inc(s_xn, 1)

            def copy_turned(k):
                act.wait_ge(s_tp, DC * k + 2)
                if k >= 2:
                    act.wait_ge(s_prj, DC * (k - 1))
                    wait(act, s_vp, GB * sources_until(k - 2))
                act.activation(turned(k)[:, 1, :], bank[1], ACT.Copy).then_inc(s_tcA, 1)

            def copy_projected(k):
                for c in range(DC):
                    s = k * DC + c
                    act.wait_ge(s_prj, s + 1)
                    if s >= FR:
                        act.wait_ge(s_lo, s - FR + 1)
                    keys = is_source(k)
                    if s == 0:
                        act.wait_ge(s_biases, 2)
                    act.activation(ring_f[:, s % FR, :], bank[2 + s % 2], ACT.Identity,
                                   bias=(kbias if keys else qbias_s)[:, c:c + 1],
                                   scale=1.0 if keys else QSCALE).then_inc(s_f, 1)
                for c in range(DC):
                    s = k * DC + c
                    act.wait_ge(s_f, s + 1)
                    if s >= FR:
                        act.wait_ge(s_parts[s % FR], 16 * (s // FR))
                    act.activation(ring_hl[:, s % FR, 0, :], ring_f[:, s % FR, :],
                                   ACT.Copy).then_inc(s_hi, 1)

            for st in range(len(STEPS) + 4):
                if 0 <= st - 3 < len(STEPS):
                    copy_turned(st - 3)
                if st < len(STEPS) and is_source(st):
                    relu(st)
                if 0 <= st - 3 < len(STEPS):
                    copy_projected(st - 3)
                if 0 <= st - 1 < len(STEPS):
                    normalise(st - 1)

            def exps(i, m):
                t, half = m // 2, m % 2
                p, c, h = m // PCH, (m % UCH) // 2, m // UCH % H
                wait(act, s_nm, i * (BCH // 2) + t + 1)
                wait(act, s_mx, i * BCH + 2 * t + 2)
                a = prob[:, (t + PR // 2) % PR, half * CH:(half + 1) * CH]
                if m % PCH == 0:
                    wait(act, s_den, i * PAIRS_IN_BODY + p - 1)
                act.activation(a, a, ACT.Exp, bias=minrow[:, t % (MR // 2):t % (MR // 2) + 1], scale=-1.0,
                               accum_out=denhalf[:, p % 2, half, c, h:h + 1]).then_inc(s_exp, 1)

            def copy_b(i, m):
                u, c, half = m // UCH, (m % UCH) // 2, m % 2
                wait(act, s_trB, i * BCH + m + 1)
                if m % UCH == 0:
                    wait(act, s_pv, i * BU + u - 1)
                act.activation(
                    probT[:, u % 2, half * 8 + 4:half * 8 + 8, c * P:(c + 1) * P],
                    trB[:].rearrange("p (s t) -> p s t", t=P), ACT.Copy).then_inc(s_evB, 1)

            def copy_context(i, u):
                wait(act, s_pv, i * BU + u + 1)
                if u % HG == 0:
                    wait(act, s_sum, i * (BU // HG) + u // HG)
                act.activation(cpart[:, u % CR, :], pv[:, 0:PAIR], ACT.Copy).then_inc(s_ctx, 1)

            def slice_(i, n, first, over):
                def lagging(lag):
                    return not (first and n < lag) and not (over and n >= lag)

                if n % UCH == 0 and lagging(CTX_LAG):
                    copy_context(i, (n - CTX_LAG) // UCH)
                if lagging(EXP_LAG):
                    exps(i, n - EXP_LAG)
                if lagging(T_LAG):
                    copy_b(i, n - T_LAG)

            for n in range(BCH):
                slice_(0, n, True, False)
            with act.Fori(1, TRIPS) as i:
                for n in range(BCH):
                    slice_(i, n, False, False)
            def copy_rden(g):
                act.wait_ge(s_rt, g + 1)
                b = g if g < 2 else 4 + g
                act.activation(rdT[:, g % 2, 0, :], bank[b][0:H, :], ACT.Copy).then_inc(s_rtc, 1)

            for n in range(CTX_LAG + 1):
                slice_(TRIPS, n, False, True)
                if n == T_LAG:
                    act.wait_ge(s_qk, NPAIR * PCH)
                    act.wait_ge(s_w1l, 16)
                    act.activation(w12h[:, 0, :], w12[:, 0, :], ACT.Copy).then_inc(s_w1s, 1)
                    act.wait_ge(s_w2l, 16)
                    act.activation(w12h[:, 1, :], w12[:, 1, :], ACT.Copy).then_inc(s_w2s, 1)
                if n == COPY_AT:
                    copy_rden(0)
                    copy_rden(1)

            def mask3(g):
                for j in range(GB):
                    act.wait_ge(s_n2, GB * g + j + 1)
                    if g >= 2:
                        act.wait_ge(s_y2, GB * (g - 1))
                    act.activation(ht2[:, g % 2 * GB + j, :], hid[:, j, :], ACT.Copy,
                                   scale=nmaskf[:, g * GB + j:g * GB + j + 1]).then_inc(s_n3, 1)

            def copy3(g):
                for c in range(DC):
                    act.wait_ge(s_t3, DC * g + c + 1)
                    if g >= 1:
                        act.wait_ge(s_f1, FC * g)
                        act.wait_ge(s_c3l, DC * g)
                    act.activation(hidTh[:, c, :], bank[2 + c], ACT.Copy).then_inc(s_c3, 1)

            def gelu(g):
                for f in range(FC):
                    act.wait_ge(s_f1, FC * g + f + 1)
                    if g >= 1:
                        act.wait_ge(s_f2, GB * g)
                    for dst in (gel[:, f, :], gelh[:, f, :]):
                        act.activation(dst, bank[4 + f % 2], ACT.Gelu_apprx_tanh).then_inc(s_g, 1)

            mask3(0)
            copy3(0)
            copy_rden(2)
            copy_rden(3)
            for g in range(NG):
                gelu(g)
                if g + 1 < NG:
                    mask3(g + 1)
                    copy3(g + 1)

        @block.vector
        def _(dve):
            count = [0]

            def moments(k, src_stats, dst, s_dst):
                b = k % 2
                for j in range(GB):
                    dve.bn_stats(src_stats[:, j, :], tokens(k)[:, j, :]).then_inc(s_stat, 1)
                count[0] += GB
                dve.wait_ge(s_stat, count[0])
                for j in range(GB):
                    dve.bn_aggr(dst[:, b, j, :], src_stats[:, j, :]).then_inc(s_dst, 1)

            def moments_x(k):
                n = sources_until(k)
                dve.wait_ge(s_xin[k], 16)
                if n > 1:
                    dve.wait_ge(s_mv1, GB * (n - 1))
                if n > 2:
                    dve.wait_ge(s_r1, n - 2)
                moments(k, stats, mv, s_mv1)

            def moments_h(k):
                if is_source(k):
                    dve.wait_ge(s_relu, GB * sources_until(k))
                else:
                    dve.wait_ge(s_xin[k], 16)
                if k >= 1:
                    dve.wait_ge(s_mv2, GB * k)
                if k >= 2:
                    dve.wait_ge(s_r2, k - 1)
                moments(k, stats2, mv2, s_mv2)

            def shift(k):
                g = STEPS[k][1]
                for j in range(GB):
                    dve.wait_ge(s_sc, GB * k + j + 1)
                    t = tokens(k)[:, j, :]
                    dve.scalar_tensor_tensor(t, b1_bc, nmaskf[:, g * GB + j:g * GB + j + 1], t,
                                             ALU.mult, ALU.add).then_inc(s_ln, 1)

            def copy_turned(k):
                dve.wait_ge(s_tp, DC * k + 1)
                if k >= 2:
                    dve.wait_ge(s_prj, DC * (k - 1))
                    wait(dve, s_vp, GB * sources_until(k - 2))
                dve.tensor_copy(turned(k)[:, 0, :], bank[0]).then_inc(s_tcD, 1)

            def low(k):
                for c in range(DC):
                    s = k * DC + c
                    dve.wait_ge(s_hi, s + 1)
                    dve.tensor_tensor(ring_hl[:, s % FR, 1, :], ring_f[:, s % FR, :],
                                      ring_hl[:, s % FR, 0, :].bitcast(F32), ALU.subtract).then_inc(s_lo, 1)

            def copy_values(k):
                g, n = STEPS[k][1], sources_until(k) - 1
                for j in range(GB):
                    dve.wait_ge(s_vp, GB * n + j + 1)
                    if n == 0 and j == 0:
                        dve.wait_ge(s_w, 64)
                    dve.tensor_tensor(vals[:, g * GB + j, :], bank[4 + j][:, 0:D], bv_bc,
                                      ALU.add).then_inc(s_ve, 1)

            dve.wait_ge(s_rowsT, 1)
            dve.wait_ge(s_biases, 2)
            dve.tensor_copy(nmaskf[:], bank[7][:, 0:NB]).then_inc(s_rowsT, 1)
            dve.wait_ge(s_const, 2)
            dve.tensor_copy(head_sel_r[:], head_sel).then_inc(s_hsel, 1)
            dve.tensor_reduce(part_sel[:], ident[:].rearrange("p (j d) -> p d j", d=HD), AX.X,
                              ALU.add).then_inc(s_psel, 1)
            dve.wait_ge(s_w1, 32)
            for st in range(len(STEPS) + 5):
                if st < len(STEPS) and is_source(st):
                    moments_x(st)
                if st == len(STEPS) + 1:
                    dve.wait_ge(s_adj0, 16)
                    m0 = mask[:, 0, :, :].rearrange("p a n -> p (a n)")
                    dve.tensor_scalar(m0, m0.bitcast(I32), 0.0, NEG, ALU.is_equal, ALU.mult).then_inc(s_m0, 1)
                if 0 <= st - 4 < len(STEPS):
                    low(st - 4)
                if 0 <= st - 4 < len(STEPS) and is_source(st - 4):
                    copy_values(st - 4)
                if 0 <= st - 3 < len(STEPS):
                    copy_turned(st - 3)
                if 0 <= st - 1 < len(STEPS):
                    moments_h(st - 1)
                if 0 <= st - 2 < len(STEPS):
                    shift(st - 2)
            dve.wait_ge(s_prj, DC * len(STEPS))

            def copy_a(i, m):
                u, c, half = m // UCH, (m % UCH) // 2, m % 2
                if m % UCH == 0:
                    wait(dve, s_pv, i * BU + u - 1)
                wait(dve, s_trA, i * BCH + m + 1)
                dve.tensor_copy(
                    probT[:, u % 2, half * 8:half * 8 + 4, c * P:(c + 1) * P],
                    trA[:].rearrange("p (s t) -> p s t", t=P)).then_inc(s_evA, 1)

            def masked_min(i, n):
                t, half = n // 2, n % 2
                p, c = n // PCH, (n % UCH) // 2
                dve.tensor_tensor_reduce(
                    out=prob[:, (t + PR // 2) % PR, half * CH:(half + 1) * CH], in0=score[n % 2][:],
                    in1=mask[:, p % 2, c, half * CH:(half + 1) * CH], scale=1.0, scalar=HUGE,
                    op0=ALU.add, op1=ALU.min, accum_out=minhalf[:, n % MR:n % MR + 1]).then_inc(s_mx, 1)

            def copy_sum(i, v):
                wait(dve, s_sum, i * (BU // HG) + v + 1)
                wait(dve, s_cst[v % 2], 16 * (i * (BU // HG // 2) + v // 2))
                dve.tensor_copy(csum[:, v % 2, :], psum_sum[:, 0:PAIR]).then_inc(s_sumc, 1)

            def denominators(i, p):
                pair = i * PAIRS_IN_BODY + p
                wait(dve, s_exp, pair * PCH + PCH)
                d = denhalf[:, p % 2, :, :, :].rearrange("p a b h -> p a (b h)")
                o = den[:].rearrange("p b h -> p (b h)")[:, bass.ds(pair * 2 * H, 2 * H)]
                dve.tensor_tensor(o, d[:, 0, :], d[:, 1, :], ALU.add).then_inc(s_den, 1)

            def slice_(i, n, first, over):
                def lagging(lag):
                    return not (first and n < lag) and not (over and n >= lag)

                if lagging(T_LAG):
                    copy_a(i, n - T_LAG)
                if (n - SUM_COPY_LAG) % SCH == 0 and lagging(SUM_COPY_LAG):
                    copy_sum(i, (n - SUM_COPY_LAG) // SCH)
                if n % PCH == DEN_AT and not (first and n < PCH) and not (over and n >= PCH):
                    denominators(i, n // PCH - 1)
                if over:
                    return
                if first:
                    if n == 0:
                        dve.wait_ge(s_m0, 1)
                    if n == PR:
                        dve.wait_ge(s_hts, 16 * NG)
                        dve.wait_ge(s_tp, DC * len(STEPS))
                    if n == PCH:
                        dve.wait_ge(s_m, 16)
                    dve.wait_ge(s_qk, n + 1)
                elif n % PCH == 0:
                    dve.wait_ge(s_m, 16 * (i * PAIRS_IN_BODY + n // PCH))
                    dve.nop(nofuse=True)
                masked_min(i, n)

            for n in range(BCH):
                slice_(0, n, True, False)
            with dve.Fori(1, TRIPS) as i:
                for n in range(BCH):
                    slice_(i, n, False, False)
            def reciprocals(b0, b1):
                dve.reciprocal(rden[:, b0:b1, :], den[:, b0:b1, :]).then_inc(s_rd, 1)

            def rden_low(g):
                dve.wait_ge(s_rtc, g + 1)
                b = g if g < 2 else 4 + g
                dve.tensor_tensor(rdT[:, g % 2, 1, :], bank[b][0:H, :], rdT[:, g % 2, 0, :].bitcast(F32),
                                  ALU.subtract).then_inc(s_rtl, 1)

            def normalise(g):
                dve.wait_ge(s_cin[g], 16)
                for c in range(DC):
                    dve.wait_ge(s_rb, DC * g + c + 1)
                    dve.tensor_tensor(cins[g][:, c, :], bank[2 + c], cins[g][:, c, :],
                                      ALU.mult).then_inc(s_cn, 1)

            def middle(g):
                for j in range(GB):
                    dve.wait_ge(s_wo, GB * g + 2 * (j // 2) + 2)
                    if g == 0 and j == 0:
                        dve.wait_ge(s_w3, 16 * 3)
                    if g >= 1:
                        dve.wait_ge(s_n3, GB * g)
                    dve.tensor_tensor(hid[:, j, :], bank[j // 2][:, D * (j % 2):D * (j % 2) + D], bo_bc,
                                      ALU.add).then_inc(s_h1, 1)
                gelu_low(g - 1, 0)
                gelu_low(g - 1, 1)
                for j in range(GB):
                    dve.wait_ge(s_h1, GB * g + j + 1)
                    tb = g * GB + j
                    dve.wait_ge(s_htin, 16 * (g + 1))
                    dve.scalar_tensor_tensor(hid[:, j, :], hid[:, j, :], nmaskf[:, tb:tb + 1], htin[:, j, :],
                                             ALU.mult, ALU.add).then_inc(s_h2, 1)
                gelu_low(g - 1, 2)
                gelu_low(g - 1, 3)
                b = g % 2
                for j in range(GB):
                    dve.wait_ge(s_h2, GB * g + j + 1)
                    if g >= 1:
                        dve.wait_ge(s_mv3, GB * g)
                    dve.bn_stats(stats[:, j, :], hid[:, j, :]).then_inc(s_st3, 1)
                gelu_low(g - 1, 4)
                for j in range(GB):
                    dve.wait_ge(s_st3, GB * g + j + 1)
                    dve.bn_aggr(mv[:, b, j, :], stats[:, j, :]).then_inc(s_mv3, 1)
                gelu_low(g - 1, 5)
                gelu_low(g - 1, 6)
                gelu_low(g - 1, 7)
                dve.wait_ge(s_mv3, GB * (g + 1))
                for j in range(GB):
                    dve.scalar_tensor_tensor(hid[:, j, :], hid[:, j, :], mv[:, b, j, 0:1], s2_bc,
                                             ALU.subtract, ALU.mult).then_inc(s_n1, 1)
                dve.wait_ge(s_r3, g + 1)
                for j in range(GB):
                    dve.wait_ge(s_n1, GB * g + j + 1)
                    dve.scalar_tensor_tensor(hid[:, j, :], hid[:, j, :], rstd[:, b, j:j + 1], b2_bc,
                                             ALU.mult, ALU.add).then_inc(s_n2, 1)

            def back(g, j):
                if g >= 0:
                    dve.wait_ge(s_f2, GB * g + j + 1)
                    r = ht2[:, g % 2 * GB + j, :]
                    dve.tensor_tensor(r, bank[6 + j % 2][:, 0:D], r, ALU.add).then_inc(s_y1, 1)

            def hidden_low(g):
                for c in range(DC):
                    dve.wait_ge(s_c3, DC * g + c + 1)
                    dve.tensor_tensor(hidTl[:, c, :], bank[2 + c], hidTh[:, c, :].bitcast(F32),
                                      ALU.subtract).then_inc(s_c3l, 1)

            def gelu_low(g, f):
                if g >= 0 and f not in POOL_LOW:
                    dve.wait_ge(s_g, 2 * (FC * g + f + 1))
                    dve.tensor_tensor(gell[:, f, :], gel[:, f, :],
                                      gelh[:, f, :].bitcast(F32), ALU.subtract).then_inc(s_gl, 1)

            for n in range(SUM_COPY_LAG):
                slice_(TRIPS, n, False, True)
                if n == 0:
                    dve.wait_ge(s_den, NPAIR - 1)
                    reciprocals(0, NB - GB)
                if n == COPY_AT:
                    rden_low(0)
                    rden_low(1)
                if n == NORM_AT:
                    normalise(0)
                if n == MIDDLE_AT:
                    middle(0)

            dve.wait_ge(s_den, NPAIR)
            reciprocals(NB - GB, NB)
            normalise(1)
            hidden_low(0)
            rden_low(2)
            rden_low(3)
            for g in range(NG):
                if g + 1 < NG:
                    middle(g + 1)
                else:
                    for f in range(FC):
                        gelu_low(g, f)
                if g + 2 < NG:
                    normalise(g + 2)
                for j in range(GB - 1):
                    back(g, j)
                if g + 1 < NG:
                    hidden_low(g + 1)
                back(g, GB - 1)

        @block.tensor
        def _(pe):
            pe.wait_ge(s_ident, 1)
            pe.wait_ge(s_rows, 16 * 3)
            pe.wait_ge(s_rowsf, 1)
            pe.transpose(bank[7][:, 0:NB], nmask_r[:], ident[0:NB, 0:NB])
            pe.transpose(bank[7][:, NB:NB + 2 * DC], bias_r[:], ident[0:2 * DC, 0:2 * DC]).then_inc(s_rowsT, 1)

            def turn(k):
                for c in range(DC):
                    for j in range(GB):
                        if c == 0:
                            pe.wait_ge(s_ln, GB * k + j + 1)
                        if j == 0 and k >= 1:
                            pe.wait_ge((s_tcD, s_tcA)[c], k)
                        mm = pe.transpose(bank[c][:, j * P:(j + 1) * P], tokens(k)[:, j, c * P:(c + 1) * P],
                                          ident[:])
                    mm.then_inc(s_tp, 1)

            def project(k):
                w = wqkv[:, 1 if is_source(k) else 0, :, :]
                pe.wait_ge(s_tcD, k + 1)
                pe.wait_ge(s_tcA, k + 1)
                if k == 0:
                    pe.wait_ge(s_w, 64)
                for m in range(DC):
                    s = k * DC + m
                    if s >= 2:
                        pe.wait_ge(s_f, s - 1)
                    for c in range(DC):
                        mm = pe.matmul(bank[2 + s % 2], w[:, c, m * P:(m + 1) * P], turned(k)[:, c, :],
                                       start=(c == 0), stop=(c == DC - 1))
                    mm.then_inc(s_prj, 1)

            def project_values(k):
                n = sources_until(k) - 1
                if n == 0:
                    pe.wait_ge(s_rowsT, 2)
                    pe.wait_ge(s_biases, 2)
                for j in range(GB):
                    if n >= 1:
                        pe.wait_ge(s_ve, GB * (n - 1) + j + 1)
                    for c in range(DC):
                        mm = pe.matmul(bank[4 + j][:, 0:D], turned(k)[:, c, j * P:(j + 1) * P],
                                       wqkv[:, 2, c, :], start=(c == 0), stop=(c == DC - 1))
                    mm.then_inc(s_vp, 1)

            for k in range(len(STEPS)):
                turn(k)
                project(k)
                if is_source(k):
                    project_values(k)

            def scores(i, n):
                p, h, c, half = n // PCH, n // UCH % H, (n % UCH) // 2, n % 2
                wait(pe, s_mx, i * BCH + n - 1)
                for k in range(CH // GT):
                    at = half * CH + k * GT
                    mm = pe.matmul(score[n % 2][:, k * GT:(k + 1) * GT],
                                   qst[:, p % 2, h, c * P:(c + 1) * P], kst[:, h, at:at + GT],
                                   start=True, stop=True)
                mm.then_inc(s_qk, 1)

            def turn_probs(i, m):
                t, half = m // 2, m % 2
                wait(pe, s_exp, i * BCH + m + 1)
                for dst, s_free, s_done, b0 in ((trA, s_evA, s_trA, 0), (trB, s_evB, s_trB, 4)):
                    wait(pe, s_free, i * BCH + m)
                    for b in range(4):
                        at = (half * 8 + b0 + b) * P
                        mm = pe.transpose(dst[:, b * P:(b + 1) * P], prob[:, (t + PR // 2) % PR, at:at + P], ident[:])
                    mm.then_inc(s_done, 1)

            def context(i, u, k):
                h = u % H
                if k == 0:
                    wait(pe, s_evA, i * BCH + UCH * u + UCH)
                    wait(pe, s_evB, i * BCH + UCH * u + UCH)
                    wait(pe, s_ctx, i * BU + u)
                for j in range(HG):
                    sblk = HG * k + j
                    mm = pe.matmul(pv[HD * j:HD * (j + 1), 0:PAIR], vals[:, sblk, h * HD:(h + 1) * HD],
                                   probT[:, u % 2, sblk, :], start=(k == 0), stop=(k == NB // HG - 1))
                if k == NB // HG - 1:
                    mm.then_inc(s_pv, 1)

            def sum_parts(i, v):
                wait(pe, s_ctx, i * BU + HG * (v + 1))
                wait(pe, s_sumc, i * (BU // HG) + v)
                for j in range(HG):
                    mm = pe.matmul(psum_sum[HD * j:HD * (j + 1), 0:PAIR], part_sel[:], cpart[:, j, :],
                                   start=True, stop=True)
                mm.then_inc(s_sum, 1)

            def slice_(i, n, first, over):
                def lagging(lag):
                    return not (first and n < lag) and not (over and n >= lag)

                if not over:
                    if n % PCH == 0:
                        pe.wait_ge(s_qst[n // PCH], 64 * (i + 1))
                    scores(i, n)
                if lagging(T_LAG):
                    turn_probs(i, n - T_LAG)
                if lagging(PV_LAG):
                    context(i, (n - PV_LAG) // UCH, (n - PV_LAG) % UCH)
                if (n - SUM_LAG) % SCH == 0 and lagging(SUM_LAG):
                    sum_parts(i, (n - SUM_LAG) // SCH)

            pe.wait_ge(s_f, len(STEPS) * DC)
            pe.wait_ge(s_ve, GB * NG)
            pe.wait_ge(s_psel, 1)
            pe.wait_ge(s_kst, 64 * NG)
            for n in range(BCH):
                slice_(0, n, True, False)
            with pe.Fori(1, TRIPS) as i:
                for n in range(BCH):
                    slice_(i, n, False, False)
            def turn_rden(g):
                b = g if g < 2 else 4 + g
                for j in range(GB):
                    mm = pe.transpose(bank[b][0:H, j * P:(j + 1) * P], rden[:, g * GB + j, :], ident[:])
                mm.then_inc(s_rt, 1)

            def spread(g):
                pe.wait_ge(s_rtc, g + 1)
                if g >= 2:
                    pe.wait_ge(s_c3l, DC * (g - 1))
                pe.wait_ge(s_rtl, g + 1)
                for c in range(DC):
                    for part in range(2):
                        mm = pe.matmul(bank[2 + c], head_sel_r[:, c * P:(c + 1) * P], rdT[:, g % 2, part, :],
                                       start=(part == 0), stop=(part == 1))
                    mm.then_inc(s_rb, 1)

            def project_out(g):
                if g == 0:
                    pe.wait_ge(s_wol, 16)
                    pe.wait_ge(s_rtl, 2)
                else:
                    pe.wait_ge(s_h1, GB * g)
                pe.wait_ge(s_cn, DC * (g + 1))
                for j in range(GB):
                    for c in range(DC):
                        mm = pe.matmul(bank[j // 2][:, D * (j % 2):D * (j % 2) + D],
                                       cins[g][:, c, j * P:(j + 1) * P], wo[:, c, :],
                                       start=(c == 0), stop=(c == DC - 1))
                    mm.then_inc(s_wo, 1)

            for n in range(SUM_LAG):
                slice_(TRIPS, n, False, True)
                if n == TURN_AT:
                    pe.wait_ge(s_mx, NPAIR * PCH)
                    pe.wait_ge(s_hsel, 1)
                    pe.wait_ge(s_rd, 1)
                    turn_rden(0)
                    turn_rden(1)
                if n == SPREAD_AT:
                    spread(0)
                if n == OUT_AT:
                    project_out(0)

            pe.wait_ge(s_evA, NPAIR * PCH)
            pe.wait_ge(s_evB, NPAIR * PCH)
            pe.wait_ge(s_ctx, NPAIR * H)

            def turn3(g):
                for c in range(DC):
                    for j in range(GB):
                        if c == 0:
                            pe.wait_ge(s_n3, GB * g + j + 1)
                        if j == 0:
                            pe.wait_ge(s_cn, DC * min(g + 2, NG))
                        mm = pe.transpose(bank[2 + c][:, j * P:(j + 1) * P],
                                          ht2[:, g % 2 * GB + j, c * P:(c + 1) * P], ident[:])
                    mm.then_inc(s_t3, 1)

            def split_products(dst, w, a, first, last):
                (wh, wl), (ah, al) = w, a
                pe.matmul(dst, wh, ah, start=first, stop=False)
                pe.matmul(dst, wh, al, start=False, stop=False)
                return pe.matmul(dst, wl, ah, start=False, stop=last)

            def ffn1(g):
                pe.wait_ge(s_c3l, DC * (g + 1))
                if g == 0:
                    pe.wait_ge(s_w1s, 2)
                for f in range(FC):
                    if g * FC + f >= 2:
                        pe.wait_ge(s_g, 2 * (g * FC + f - 1))
                    for c in range(DC):
                        at = slice(f * P, (f + 1) * P)
                        mm = split_products(bank[4 + f % 2], (w1h[:, c, at], w1l[:, c, at]),
                                            (hidTh[:, c, :], hidTl[:, c, :]), c == 0, c == DC - 1)
                    mm.then_inc(s_f1, 1)

            def ffn2(g, js):
                if g == 0 and 0 in js:
                    pe.wait_ge(s_w2s, 2)
                    pe.wait_ge(s_rtc, NG)
                    pe.wait_ge(s_rtl, NG)
                for j in js:
                    if GB * g + j >= 2:
                        pe.wait_ge(s_y1, GB * g + j - 1)
                    for f in range(FC):
                        if j == 0:
                            if f in POOL_LOW:
                                pe.wait_ge(s_glp, len(POOL_LOW) * g + POOL_LOW.index(f) + 1)
                            else:
                                pe.wait_ge(s_gl, len(VECTOR_LOW) * g + VECTOR_LOW.index(f) + 1)
                        at = slice(j * P, (j + 1) * P)
                        mm = split_products(bank[6 + j % 2][:, 0:D],
                                            (gelh[:, f, at], gell[:, f, at]),
                                            (w2h[:, f, :], w2l[:, f, :]), f == 0, f == FC - 1)
                    mm.then_inc(s_f2, 1)

            spread(1)
            turn3(0)
            project_out(1)
            pe.wait_ge(s_sumc, NPAIR * DC)
            pe.wait_ge(s_rd, 2)
            turn_rden(2)
            turn_rden(3)
            for g in range(NG):
                ffn1(g)
                if g + 2 < NG:
                    spread(g + 2)
                ffn2(g, range(GB - 1))
                if g + 1 < NG:
                    turn3(g + 1)
                ffn2(g, (GB - 1,))
                if g + 2 < NG:
                    project_out(g + 2)


_INS = ["x", "adj", "nodemask", "L0_gnn_h_target", "L0_gnn_ln1_scale", "L0_gnn_ln1_bias",
        "L0_gnn_Wq", "L0_gnn_bq", "L0_gnn_Wk", "L0_gnn_bk", "L0_gnn_Wv", "L0_gnn_bv", "L0_gnn_Wo",
        "L0_gnn_bo", "L0_gnn_ln2_scale", "L0_gnn_ln2_bias", "L0_gnn_W1", "L0_gnn_W2"]


def kernel(**inputs):
    import numpy as np
    import concourse.bacc as bacc
    from concourse.bass_utils import run_bass_kernel_spmd

    nc = bacc.Bacc("TRN2", target_bir_lowering=False, num_devices=1)
    arrays, args = {}, []
    for name in _INS:
        a = np.ascontiguousarray(inputs[name])
        arrays[f"in_{name}"] = a
        args.append(nc.dram_tensor(f"in_{name}", a.shape, mybir.dt.from_np(a.dtype), kind="ExternalInput").ap())
    out = nc.dram_tensor("out_0", (N, D), F32, kind="ExternalOutput").ap()
    program(nc, *args, out)
    r = run_bass_kernel_spmd(nc, [arrays], core_ids=[0])
    return r.results[0]["out_0"]
```
